# Optimizing a Trainium2 kernel written in Bass

```python
import numpy as np
import jax
import jax.numpy as jnp

def _softmax(x, axis=-1):
    return jax.nn.softmax(x, axis=axis)
def _gelu(x):
    return jax.nn.gelu(x, approximate=True)
def _silu(x):
    return jax.nn.silu(x)
def _sigmoid(x):
    return jax.nn.sigmoid(x)
def _layernorm(x, axis=-1, eps=1e-5):
    m = jnp.mean(x, axis=axis, keepdims=True)
    v = jnp.var(x, axis=axis, keepdims=True)
    return (x - m) / jnp.sqrt(v + eps)
def _scatter_add(tgt, idx, src, axis=0):
    return tgt.at[idx].add(src)
def _segment_sum(src, seg, n):
    return jax.ops.segment_sum(src, seg, n)

kernel_name = 'mk_conv_seq_d2_conv_nhwc512_609606'

def setup_inputs(seed: int = 0):
    np.random.seed(seed)
    _w = jnp.asarray
    def _rec_inputs():
        import jax
        import jax.numpy as jnp
        _gk = jax.random.key(seed)
        x = -8.268e-05 + 0.9999 * jax.random.normal(jax.random.fold_in(_gk, 1), (32, 56, 56, 512), jnp.float32)
        return x
    x = _rec_inputs()
    def _L0_conv_setup():
        import jax, jax.numpy as jnp
        import numpy as np
        EPS = 0.001
        G = 8

        def bn(x, gamma, beta, mean, var):
            return gamma * (x - mean) * jax.lax.rsqrt(var + EPS) + beta

        def group_conv1x1(x, w, b):
            n, h, wd, c = x.shape
            g = w.shape[0]
            xg = x.reshape(n, h, wd, g, c // g)
            y = jnp.einsum('nhwgc,gcd->nhwgd', xg, w)
            return y.reshape(n, h, wd, -1) + b

        def channel_shuffle(x, g):
            n, h, w, c = x.shape
            return x.reshape(n, h, w, g, c // g).transpose(0, 1, 2, 4, 3).reshape(n, h, w, c)

        def depthwise3x3(x, w, b):
            c = x.shape[-1]
            y = jax.lax.conv_general_dilated(x, w, window_strides=(1, 1), padding='SAME', dimension_numbers=('NHWC', 'HWIO', 'NHWC'), feature_group_count=c)
            return y + b
        key = jax.random.key(seed)
        ks = jax.random.split(key, 4)
        N, H, W, C = (32, 56, 56, 512)
        B = C // 4
        d = {'x': jax.random.normal(ks[0], (N, H, W, C), jnp.float32), 'w1': jax.random.normal(ks[1], (G, C // G, B // G), jnp.float32) * 0.05, 'b1': jnp.zeros((B,), jnp.float32), 'dw_w': jax.random.normal(ks[2], (3, 3, 1, B), jnp.float32) * 0.05, 'dw_b': jnp.zeros((B,), jnp.float32), 'w2': jax.random.normal(ks[3], (G, B // G, C // G), jnp.float32) * 0.05, 'b2': jnp.zeros((C,), jnp.float32)}
        for i, ch in [(1, B), (2, B), (3, B), (4, C)]:
            d[f'bn{i}_g'] = jnp.ones((ch,), jnp.float32)
            d[f'bn{i}_b'] = jnp.zeros((ch,), jnp.float32)
            d[f'bn{i}_m'] = jnp.zeros((ch,), jnp.float32)
            d[f'bn{i}_v'] = jnp.ones((ch,), jnp.float32)
        return d
    _L0_conv_all = _L0_conv_setup()
    _L0_conv_in = {k: v for k, v in _L0_conv_all.items() if k in ('w1', 'b1', 'bn1_g', 'bn1_b', 'bn1_m', 'bn1_v', 'dw_w', 'dw_b', 'bn2_g', 'bn2_b', 'bn2_m', 'bn2_v', 'bn3_g', 'bn3_b', 'bn3_m', 'bn3_v', 'w2', 'b2', 'bn4_g', 'bn4_b', 'bn4_m', 'bn4_v', )}
    del _L0_conv_all

    def _L1_conv_setup():
        import jax, jax.numpy as jnp
        import numpy as np
        EPS = 0.001
        G = 8

        def bn(x, gamma, beta, mean, var):
            return gamma * (x - mean) * jax.lax.rsqrt(var + EPS) + beta

        def group_conv1x1(x, w, b):
            n, h, wd, c = x.shape
            g = w.shape[0]
            xg = x.reshape(n, h, wd, g, c // g)
            y = jnp.einsum('nhwgc,gcd->nhwgd', xg, w)
            return y.reshape(n, h, wd, -1) + b

        def channel_shuffle(x, g):
            n, h, w, c = x.shape
            return x.reshape(n, h, w, g, c // g).transpose(0, 1, 2, 4, 3).reshape(n, h, w, c)

        def depthwise3x3(x, w, b):
            c = x.shape[-1]
            y = jax.lax.conv_general_dilated(x, w, window_strides=(1, 1), padding='SAME', dimension_numbers=('NHWC', 'HWIO', 'NHWC'), feature_group_count=c)
            return y + b
        key = jax.random.key(seed)
        ks = jax.random.split(key, 4)
        N, H, W, C = (32, 56, 56, 512)
        B = C // 4
        d = {'x': jax.random.normal(ks[0], (N, H, W, C), jnp.float32), 'w1': jax.random.normal(ks[1], (G, C // G, B // G), jnp.float32) * 0.05, 'b1': jnp.zeros((B,), jnp.float32), 'dw_w': jax.random.normal(ks[2], (3, 3, 1, B), jnp.float32) * 0.05, 'dw_b': jnp.zeros((B,), jnp.float32), 'w2': jax.random.normal(ks[3], (G, B // G, C // G), jnp.float32) * 0.05, 'b2': jnp.zeros((C,), jnp.float32)}
        for i, ch in [(1, B), (2, B), (3, B), (4, C)]:
            d[f'bn{i}_g'] = jnp.ones((ch,), jnp.float32)
            d[f'bn{i}_b'] = jnp.zeros((ch,), jnp.float32)
            d[f'bn{i}_m'] = jnp.zeros((ch,), jnp.float32)
            d[f'bn{i}_v'] = jnp.ones((ch,), jnp.float32)
        return d
    _L1_conv_all = _L1_conv_setup()
    _L1_conv_in = {k: v for k, v in _L1_conv_all.items() if k in ('w1', 'b1', 'bn1_g', 'bn1_b', 'bn1_m', 'bn1_v', 'dw_w', 'dw_b', 'bn2_g', 'bn2_b', 'bn2_m', 'bn2_v', 'bn3_g', 'bn3_b', 'bn3_m', 'bn3_v', 'w2', 'b2', 'bn4_g', 'bn4_b', 'bn4_m', 'bn4_v', )}
    del _L1_conv_all

    return {
        "x": x,
        "L0_conv_w1": _L0_conv_in["w1"],
        "L0_conv_b1": _L0_conv_in["b1"],
        "L0_conv_bn1_g": _L0_conv_in["bn1_g"],
        "L0_conv_bn1_b": _L0_conv_in["bn1_b"],
        "L0_conv_bn1_m": _L0_conv_in["bn1_m"],
        "L0_conv_bn1_v": _L0_conv_in["bn1_v"],
        "L0_conv_dw_w": _L0_conv_in["dw_w"],
        "L0_conv_dw_b": _L0_conv_in["dw_b"],
        "L0_conv_bn2_g": _L0_conv_in["bn2_g"],
        "L0_conv_bn2_b": _L0_conv_in["bn2_b"],
        "L0_conv_bn2_m": _L0_conv_in["bn2_m"],
        "L0_conv_bn2_v": _L0_conv_in["bn2_v"],
        "L0_conv_bn3_g": _L0_conv_in["bn3_g"],
        "L0_conv_bn3_b": _L0_conv_in["bn3_b"],
        "L0_conv_bn3_m": _L0_conv_in["bn3_m"],
        "L0_conv_bn3_v": _L0_conv_in["bn3_v"],
        "L0_conv_w2": _L0_conv_in["w2"],
        "L0_conv_b2": _L0_conv_in["b2"],
        "L0_conv_bn4_g": _L0_conv_in["bn4_g"],
        "L0_conv_bn4_b": _L0_conv_in["bn4_b"],
        "L0_conv_bn4_m": _L0_conv_in["bn4_m"],
        "L0_conv_bn4_v": _L0_conv_in["bn4_v"],
        "L1_conv_w1": _L1_conv_in["w1"],
        "L1_conv_b1": _L1_conv_in["b1"],
        "L1_conv_bn1_g": _L1_conv_in["bn1_g"],
        "L1_conv_bn1_b": _L1_conv_in["bn1_b"],
        "L1_conv_bn1_m": _L1_conv_in["bn1_m"],
        "L1_conv_bn1_v": _L1_conv_in["bn1_v"],
        "L1_conv_dw_w": _L1_conv_in["dw_w"],
        "L1_conv_dw_b": _L1_conv_in["dw_b"],
        "L1_conv_bn2_g": _L1_conv_in["bn2_g"],
        "L1_conv_bn2_b": _L1_conv_in["bn2_b"],
        "L1_conv_bn2_m": _L1_conv_in["bn2_m"],
        "L1_conv_bn2_v": _L1_conv_in["bn2_v"],
        "L1_conv_bn3_g": _L1_conv_in["bn3_g"],
        "L1_conv_bn3_b": _L1_conv_in["bn3_b"],
        "L1_conv_bn3_m": _L1_conv_in["bn3_m"],
        "L1_conv_bn3_v": _L1_conv_in["bn3_v"],
        "L1_conv_w2": _L1_conv_in["w2"],
        "L1_conv_b2": _L1_conv_in["b2"],
        "L1_conv_bn4_g": _L1_conv_in["bn4_g"],
        "L1_conv_bn4_b": _L1_conv_in["bn4_b"],
        "L1_conv_bn4_m": _L1_conv_in["bn4_m"],
        "L1_conv_bn4_v": _L1_conv_in["bn4_v"],
    }

def reference(x, L0_conv_w1, L0_conv_b1, L0_conv_bn1_g, L0_conv_bn1_b, L0_conv_bn1_m, L0_conv_bn1_v, L0_conv_dw_w, L0_conv_dw_b, L0_conv_bn2_g, L0_conv_bn2_b, L0_conv_bn2_m, L0_conv_bn2_v, L0_conv_bn3_g, L0_conv_bn3_b, L0_conv_bn3_m, L0_conv_bn3_v, L0_conv_w2, L0_conv_b2, L0_conv_bn4_g, L0_conv_bn4_b, L0_conv_bn4_m, L0_conv_bn4_v, L1_conv_w1, L1_conv_b1, L1_conv_bn1_g, L1_conv_bn1_b, L1_conv_bn1_m, L1_conv_bn1_v, L1_conv_dw_w, L1_conv_dw_b, L1_conv_bn2_g, L1_conv_bn2_b, L1_conv_bn2_m, L1_conv_bn2_v, L1_conv_bn3_g, L1_conv_bn3_b, L1_conv_bn3_m, L1_conv_bn3_v, L1_conv_w2, L1_conv_b2, L1_conv_bn4_g, L1_conv_bn4_b, L1_conv_bn4_m, L1_conv_bn4_v):
    import jax
    import jax.numpy as jnp
    def _L0_conv_ref(x, w1, b1, bn1_g, bn1_b, bn1_m, bn1_v, dw_w, dw_b, bn2_g, bn2_b, bn2_m, bn2_v, bn3_g, bn3_b, bn3_m, bn3_v, w2, b2, bn4_g, bn4_b, bn4_m, bn4_v):
        import jax, jax.numpy as jnp
        import numpy as np
        EPS = 0.001
        G = 8

        def bn(x, gamma, beta, mean, var):
            return gamma * (x - mean) * jax.lax.rsqrt(var + EPS) + beta

        def group_conv1x1(x, w, b):
            n, h, wd, c = x.shape
            g = w.shape[0]
            xg = x.reshape(n, h, wd, g, c // g)
            y = jnp.einsum('nhwgc,gcd->nhwgd', xg, w)
            return y.reshape(n, h, wd, -1) + b

        def channel_shuffle(x, g):
            n, h, w, c = x.shape
            return x.reshape(n, h, w, g, c // g).transpose(0, 1, 2, 4, 3).reshape(n, h, w, c)

        def depthwise3x3(x, w, b):
            c = x.shape[-1]
            y = jax.lax.conv_general_dilated(x, w, window_strides=(1, 1), padding='SAME', dimension_numbers=('NHWC', 'HWIO', 'NHWC'), feature_group_count=c)
            return y + b
        h = group_conv1x1(x, w1, b1)
        h = jax.nn.relu(bn(h, bn1_g, bn1_b, bn1_m, bn1_v))
        h = channel_shuffle(h, G)
        h = bn(depthwise3x3(h, dw_w, dw_b), bn2_g, bn2_b, bn2_m, bn2_v)
        h = bn(h, bn3_g, bn3_b, bn3_m, bn3_v)
        h = bn(group_conv1x1(h, w2, b2), bn4_g, bn4_b, bn4_m, bn4_v)
        return jax.nn.relu(x + h)

    def _L1_conv_ref(x, w1, b1, bn1_g, bn1_b, bn1_m, bn1_v, dw_w, dw_b, bn2_g, bn2_b, bn2_m, bn2_v, bn3_g, bn3_b, bn3_m, bn3_v, w2, b2, bn4_g, bn4_b, bn4_m, bn4_v):
        import jax, jax.numpy as jnp
        import numpy as np
        EPS = 0.001
        G = 8

        def bn(x, gamma, beta, mean, var):
            return gamma * (x - mean) * jax.lax.rsqrt(var + EPS) + beta

        def group_conv1x1(x, w, b):
            n, h, wd, c = x.shape
            g = w.shape[0]
            xg = x.reshape(n, h, wd, g, c // g)
            y = jnp.einsum('nhwgc,gcd->nhwgd', xg, w)
            return y.reshape(n, h, wd, -1) + b

        def channel_shuffle(x, g):
            n, h, w, c = x.shape
            return x.reshape(n, h, w, g, c // g).transpose(0, 1, 2, 4, 3).reshape(n, h, w, c)

        def depthwise3x3(x, w, b):
            c = x.shape[-1]
            y = jax.lax.conv_general_dilated(x, w, window_strides=(1, 1), padding='SAME', dimension_numbers=('NHWC', 'HWIO', 'NHWC'), feature_group_count=c)
            return y + b
        h = group_conv1x1(x, w1, b1)
        h = jax.nn.relu(bn(h, bn1_g, bn1_b, bn1_m, bn1_v))
        h = channel_shuffle(h, G)
        h = bn(depthwise3x3(h, dw_w, dw_b), bn2_g, bn2_b, bn2_m, bn2_v)
        h = bn(h, bn3_g, bn3_b, bn3_m, bn3_v)
        h = bn(group_conv1x1(h, w2, b2), bn4_g, bn4_b, bn4_m, bn4_v)
        return jax.nn.relu(x + h)

    def _gn(v, G=32, eps=1e-5):
        B_, H_, W_, C_ = v.shape
        g = v.reshape(B_, H_, W_, G, C_ // G)
        m = jnp.mean(g, axis=(1, 2, 4), keepdims=True)
        s = jnp.var(g, axis=(1, 2, 4), keepdims=True)
        return ((g - m) / jnp.sqrt(s + eps)).reshape(v.shape)

    def _ln_c(v, eps=1e-6):
        m = jnp.mean(v, axis=-1, keepdims=True)
        s = jnp.var(v, axis=-1, keepdims=True)
        return (v - m) / jnp.sqrt(s + eps)

    def _ln_t(v, eps=1e-5):
        m = jnp.mean(v, axis=-1, keepdims=True)
        s = jnp.var(v, axis=-1, keepdims=True)
        return (v - m) / jnp.sqrt(s + eps)

    def _to_tokens(v):
        B_, H_, W_, C_ = v.shape
        return v.reshape(B_, H_ * W_, C_)
    def _from_tokens(t, like):
        return t.reshape(like.shape)

    x = _L0_conv_ref(x, L0_conv_w1, L0_conv_b1, L0_conv_bn1_g, L0_conv_bn1_b, L0_conv_bn1_m, L0_conv_bn1_v, L0_conv_dw_w, L0_conv_dw_b, L0_conv_bn2_g, L0_conv_bn2_b, L0_conv_bn2_m, L0_conv_bn2_v, L0_conv_bn3_g, L0_conv_bn3_b, L0_conv_bn3_m, L0_conv_bn3_v, L0_conv_w2, L0_conv_b2, L0_conv_bn4_g, L0_conv_bn4_b, L0_conv_bn4_m, L0_conv_bn4_v)
    x = _L1_conv_ref(x, L1_conv_w1, L1_conv_b1, L1_conv_bn1_g, L1_conv_bn1_b, L1_conv_bn1_m, L1_conv_bn1_v, L1_conv_dw_w, L1_conv_dw_b, L1_conv_bn2_g, L1_conv_bn2_b, L1_conv_bn2_m, L1_conv_bn2_v, L1_conv_bn3_g, L1_conv_bn3_b, L1_conv_bn3_m, L1_conv_bn3_v, L1_conv_w2, L1_conv_b2, L1_conv_bn4_g, L1_conv_bn4_b, L1_conv_bn4_m, L1_conv_bn4_v)
    return x


_drawn_inputs = setup_inputs


def setup_inputs(seed=0):
    import zlib

    import numpy as np

    out = dict(_drawn_inputs(seed))
    spreads = {'L0_conv_b1': (0.0, 0.8),
     'L0_conv_bn1_g': (1.0, 0.6),
     'L0_conv_bn1_b': (0.0, 0.8),
     'L0_conv_bn1_m': (0.0, 0.8),
     'L0_conv_bn1_v': (1.0, 0.6),
     'L0_conv_dw_b': (0.0, 0.392),
     'L0_conv_bn2_g': (1.0, 0.6),
     'L0_conv_bn2_b': (0.0, 0.369),
     'L0_conv_bn2_m': (0.0, 0.366),
     'L0_conv_bn2_v': (1.0, 0.6),
     'L0_conv_bn3_g': (1.0, 0.6),
     'L0_conv_bn3_b': (0.0, 0.486),
     'L0_conv_bn3_m': (0.0, 0.362),
     'L0_conv_bn3_v': (1.0, 0.6),
     'L0_conv_b2': (0.0, 0.1),
     'L0_conv_bn4_g': (1.0, 0.6),
     'L0_conv_bn4_b': (0.0, 0.1),
     'L0_conv_bn4_m': (0.0, 0.1),
     'L0_conv_bn4_v': (1.0, 0.6),
     'L1_conv_b1': (0.0, 0.8),
     'L1_conv_bn1_g': (1.0, 0.6),
     'L1_conv_bn1_b': (0.0, 0.8),
     'L1_conv_bn1_m': (0.0, 0.8),
     'L1_conv_bn1_v': (1.0, 0.6),
     'L1_conv_dw_b': (0.0, 0.323),
     'L1_conv_bn2_g': (1.0, 0.6),
     'L1_conv_bn2_b': (0.0, 0.327),
     'L1_conv_bn2_m': (0.0, 0.294),
     'L1_conv_bn2_v': (1.0, 0.6),
     'L1_conv_bn3_g': (1.0, 0.6),
     'L1_conv_bn3_b': (0.0, 1.025),
     'L1_conv_bn3_m': (0.0, 0.302),
     'L1_conv_bn3_v': (1.0, 0.6),
     'L1_conv_b2': (0.0, 0.1),
     'L1_conv_bn4_g': (1.0, 0.2),
     'L1_conv_bn4_b': (0.0, 0.1),
     'L1_conv_bn4_m': (0.0, 0.1),
     'L1_conv_bn4_v': (1.0, 0.6)}
    factors = {'L0_conv_w1': 7.144, 'L0_conv_dw_w': 5.494, 'L1_conv_w1': 7.416, 'L1_conv_dw_w': 5.712}
    for name, (base, spread) in spreads.items():
        noise = np.random.default_rng([zlib.crc32(name.encode()), seed]).standard_normal(out[name].shape)
        drawn = base * np.exp(spread * noise) if base else spread * noise
        out[name] = jnp.asarray(drawn.astype(out[name].dtype))
    for name, factor in factors.items():
        out[name] = (out[name] * factor).astype(out[name].dtype)
    return out
```

```python
from contextlib import ExitStack

import numpy as np

import concourse.bass as bass
from concourse import mybir

ALU = mybir.AluOpType
ACT = mybir.ActivationFunctionType
F32 = mybir.dt.float32
F32R = mybir.dt.float32r

LAYERS = 2
IMAGES, H, W, C = 32, 56, 56, 512
GROUPS = 8
HID = C // 4
EPS = 1e-3
P = 128

UNITS = 4
ROWS = H // UNITS
TILE = 2 * W
TILES = ROWS // 2
UPIX = ROWS * W
PARTS = ((0, 4), (4, 3))
CHUNKS = C // P
PW, PH = W + 2, H + 2
TOTAL = IMAGES * UNITS

LAG_DW0, LAG_MID, LAG_DW1, LAG_OUT = 1, 2, 4, 6
PEELED = -(-LAG_OUT // UNITS)

BN = 3 + CHUNKS
NBN = LAYERS * BN
TAPS = 9
COLS = 5 * NBN + LAYERS * TAPS
ROWLEN = LAYERS * (HID + C)


def conv_stack_kernel(nc, x, cols, gamma_row, var_row, w1, w2, masks, ident, out):
    x_v = x.rearrange("n (u t r) w c -> (n u) (r w) t c", u=UNITS, t=TILES)
    out_v = out.rearrange("n (u t r) w c -> (n u) (r w) t c", u=UNITS, t=TILES)

    with ExitStack() as ctx:
        def sb(name, shape, dt=F32):
            return ctx.enter_context(nc.sbuf_tensor(name, shape, dt))

        def sem(name):
            return ctx.enter_context(nc.semaphore(name))

        x_sb = sb("x_sb", [TILE, UNITS, TILES, C])
        xt_sb = sb("xt_sb", [P, CHUNKS, UPIX])
        h_sb = [sb(f"h{n}_sb", [P, PH, PW]) for n in range(LAYERS)]
        acc_sb = [sb(f"acc{n}_sb", [P, ROWS, W]) for n in range(LAYERS)]
        q_hi = [sb(f"q{n}_hi", [P, n + 1, UPIX], F32R) for n in range(LAYERS)]
        q_lo = [sb(f"q{n}_lo", [P, n + 1, UPIX], F32R) for n in range(LAYERS)]
        mid_sb = sb("mid_sb", [P, UNITS, CHUNKS, UPIX])
        out_sb = sb("out_sb", [P, 2, TILES, C])
        ident_sb = sb("ident_sb", [P, P])
        cols_sb = sb("cols_sb", [P, COLS])
        w1_sb = sb("w1_sb", [P, LAYERS, CHUNKS, HID // CHUNKS])
        w2_hi = sb("w2_hi", [P, LAYERS, C], F32R)
        w2_lo = sb("w2_lo", [P, LAYERS, C], F32R)
        scale_c = sb("scale_c", [P, NBN])
        shift_c = sb("shift_c", [P, NBN])
        tmp_c = sb("tmp_c", [P, NBN])
        taps_sb = sb("taps_sb", [P, LAYERS, TAPS])
        beta_sb = sb("beta_sb", [P, LAYERS])
        bias4_sb = sb("bias4_sb", [P, LAYERS, CHUNKS])
        scratch = out_sb[:, :, :, :].rearrange("p s t c -> p (s t c)")
        place = [0]

        def carve(n):
            place[0] += n
            return scratch[:, place[0] - n:place[0]]

        var_all, gamma_all, root_all, inv_all = (carve(NBN + ROWLEN) for _ in range(4))
        w2_in, masks_in = carve(LAYERS * C // GROUPS), carve(GROUPS)
        w2_f = carve(C)
        w1_f = carve(LAYERS * HID)
        scale_r = inv_all[:, NBN:]

        ps = ctx.enter_context(nc.psum_tensor("ps", [P, 8, 512], F32))

        x_loaded = [[sem(f"x_loaded_{u}_{part}") for part in range(2)] for u in range(UNITS)]
        params_loaded = sem("params_loaded")
        prep = sem("prep")
        roots = sem("roots")
        bias_sums = sem("bias_sums")
        w2_placed = sem("w2_placed")
        w2_split = sem("w2_split")
        borders = sem("borders")
        blocks = sem("blocks")
        t0_filled = sem("t0_filled")
        xt_ready = sem("xt_ready")
        c1_filled = [sem(f"c1_{n}_filled") for n in range(LAYERS)]
        h_ready = [sem(f"h{n}_ready") for n in range(LAYERS)]
        taps_done = [sem(f"taps{n}_done") for n in range(LAYERS)]
        qh_ready = [sem(f"q{n}_hi_ready") for n in range(LAYERS)]
        ql_ready = [sem(f"q{n}_lo_ready") for n in range(LAYERS)]
        mid_filled = sem("mid_filled")
        mid_ready = sem("mid_ready")
        mid_biased = sem("mid_biased")
        o_filled = sem("o_filled")
        o_ready = sem("o_ready")
        stored = [[sem(f"stored_{s}_{part}") for part in range(2)] for s in range(2)]

        PREP_STEPS = 64

        def span(part):
            first, n = PARTS[part]
            return first * TILE, (first + n) * TILE

        def active(s, lag):
            return not isinstance(s, int) or 0 <= s - lag < TOTAL

        def run_steps(eng, step, last):
            for s in range(PEELED * UNITS):
                step(s, s % UNITS, s // UNITS)
            with_tail = (last - TOTAL) // UNITS if last < TOTAL else 0
            end = IMAGES + with_tail
            with eng.Fori(PEELED, end) as i:
                for u in range(UNITS):
                    step(UNITS * i + u, u, i)
            for s in range(end * UNITS, TOTAL + LAG_OUT):
                step(s, s % UNITS, s // UNITS)

        block = ctx.enter_context(nc.Block())

        @block.sync
        def _(sp):
            def load(v, u):
                for part, (t, n) in enumerate(PARTS):
                    sp.dma_start(x_sb[:, u, t:t + n, :], x_v[v][:, t:t + n, :]).then_inc(x_loaded[u][part], 16)

            sp.dma_start(ident_sb[:, :], ident).then_inc(params_loaded, 16)
            load(0, 0)
            sp.dma_start(cols_sb[:, :], cols).then_inc(params_loaded, 16)
            sp.dma_start(var_all[:, NBN:], var_row.partition_broadcast(P)).then_inc(params_loaded, 16)
            sp.dma_start(gamma_all[:, NBN:], gamma_row.partition_broadcast(P)).then_inc(params_loaded, 16)
            sp.dma_start(w2_in, w2).then_inc(params_loaded, 16)
            sp.dma_start(masks_in, masks).then_inc(params_loaded, 16)
            sp.wait_ge(blocks, 1)
            half = P // 2
            w1_f4 = w1_f.rearrange("p (l c m) -> p l c m", l=LAYERS, c=CHUNKS)
            for l in range(LAYERS):
                for t in range(2):
                    src = w1[l].rearrange("(c t) k d -> t k c d", t=2)[t]
                    sp.dma_start(w1_f4[half * t:half * (t + 1), l, :, 16 * t:16 * (t + 1)], src)\
                      .then_inc(params_loaded, 16)
            load(1, 1)

            def store(z, s, u, part):
                sp.wait_ge(o_ready, TILES * z + PARTS[part][0] + PARTS[part][1])
                t, n = PARTS[part]
                sp.dma_start(out_v[z][:, t:t + n, :], out_sb[0:TILE, s, t:t + n, :]).then_inc(stored[s][part], 16)

            def step(s, u, i):
                if active(s, LAG_OUT):
                    store(s - LAG_OUT, u % 2, u, 0)
                if active(s, -2):
                    if active(s, LAG_MID):
                        sp.wait_ge(mid_filled, 8 * (s - LAG_MID + 1))
                    load(s + 2, (u + 2) % UNITS)
                if active(s, LAG_OUT):
                    store(s - LAG_OUT, u % 2, u, 1)

            run_steps(sp, step, TOTAL - UNITS)
            for s in range(2):
                for part in range(2):
                    sp.wait_ge(stored[s][part], 16 * (TOTAL // 2))

        @block.gpsimd
        def _(pool):
            w1_zero = w1_f
            nc.gpsimd.memset(w1_zero, 0.0).then_inc(blocks, 1)
            for n in range(LAYERS):
                nc.gpsimd.memset(h_sb[n][:, :, :], 0.0).then_inc(borders, 1)

        @block.tensor
        def _(pe):
            pe.wait_ge(params_loaded, 16 * (6 + 2 * LAYERS))

            def bias_matmuls():
                for l in range(LAYERS):
                    pe.wait_ge(prep, PREP_STEPS + 2 * l + 1)
                    for c in range(CHUNKS):
                        mm = pe.matmul(ps[:, 4 + l, c:c + 1], w2_f[:, P * c:P * (c + 1)], beta_sb[:, l:l + 1],
                                       start=True, stop=True, skip_group_check=True)
                    mm.then_inc(bias_sums, 1)

            def transpose_item(s, u, i, j):
                part, cp = divmod(j, 2)
                if cp == 0:
                    pe.wait_ge(x_loaded[u][part], 16 * (i + 1))
                if j >= 2:
                    pe.wait_ge(xt_ready, 4 * s + j - 1)
                elif active(s, LAG_MID + 1):
                    pe.wait_ge(mid_ready, 8 * (s - LAG_MID - 1) + 2 * (j + 3))
                elif active(s, 1):
                    pe.wait_ge(xt_ready, 4 * (s - 1) + j + 3)
                first, n = PARTS[part]
                for k in range(2):
                    c = 2 * cp + k
                    for t in range(n):
                        tr = pe.transpose(ps[:, 2 * (j % 2) + k, TILE * t:TILE * (t + 1)],
                                          x_sb[:, u, first + t, P * c:P * (c + 1)], ident_sb[0:TILE, 0:TILE])
                tr.then_inc(t0_filled, 1)

            def conv1(n, v, part, src, ready, per_part, bank_free):
                pe.wait_ge(ready, 2 * per_part * v + per_part * (part + 1))
                if bank_free is not None:
                    pe.wait_ge(bank_free[0], bank_free[1] + part + 1)
                a, b = span(part)
                for c in range(CHUNKS):
                    mm = pe.matmul(ps[32 * c:32 * (c + 1), 6 + part, 0:b - a], w1_sb[:, n, c, :],
                                   src[:, c, a:b], start=True, stop=True)
                mm.then_inc(c1_filled[n], 1)

            def conv1_mid(s, u, part, lag):
                w = s - lag
                if active(s, lag - LAG_MID):
                    free = (h_ready[0], 2 * (s - lag + LAG_MID))
                else:
                    free = (h_ready[1], 2 * (w - 1))
                conv1(1, w, part, mid_sb[:, (u - lag) % UNITS, :, :], mid_ready, 4, free)

            def mid_item(s, u, j):
                w = s - LAG_MID
                uw = (u - LAG_MID) % UNITS
                part, cp = divmod(j, 2)
                if j == 0:
                    pe.wait_ge(ql_ready[0], w + 1)
                if j >= 2:
                    pe.wait_ge(mid_ready, 8 * w + 2 * (j - 1))
                elif active(s, 0):
                    pe.wait_ge(xt_ready, 4 * s + j + 3)
                else:
                    pe.wait_ge(mid_ready, 8 * (w - 1) + 2 * (j + 3))
                a, b = span(part)
                first, n = PARTS[part]
                for k in range(2):
                    c = 2 * cp + k
                    bank = 2 * (j % 2) + k
                    for m, (wt, q) in enumerate(((w2_hi, q_hi[0]), (w2_lo, q_hi[0]), (w2_hi, q_lo[0]))):
                        pe.matmul(ps[:, bank, 0:b - a], wt[:, 0, P * c:P * (c + 1)], q[:, 0, a:b],
                                  start=(m == 0), stop=(m == 2))
                    for t in range(n):
                        tr = pe.matmul(ps[:, bank, TILE * t:TILE * (t + 1)],
                                       x_sb[:, uw, first + t, P * c:P * (c + 1)], ident_sb[0:TILE, 0:TILE],
                                       start=False, stop=True, is_transpose=True, skip_group_check=True)
                    tr.then_inc(mid_filled, 1)

            def out_tile(s, u, t):
                z = s - LAG_OUT
                uz = (u - LAG_OUT) % UNITS
                bank = 4 + (u + t) % 2
                if t == 0:
                    pe.wait_ge(ql_ready[1], z + 1)
                    pe.wait_ge(mid_biased, 4 * (z + 1))
                if not isinstance(z, int) or z > 0 or t >= 2:
                    pe.wait_ge(o_ready, TILES * z + t - 1)
                cut = slice(TILE * t, TILE * (t + 1))
                for m, (q, wt) in enumerate(((q_hi[1], w2_hi), (q_hi[1], w2_lo), (q_lo[1], w2_hi))):
                    pe.matmul(ps[0:TILE, bank, :], q[:, uz % 2, cut], wt[:, 1, :], start=(m == 0), stop=(m == 2))
                for c in range(CHUNKS):
                    tr = pe.matmul(ps[0:TILE, bank, P * c:P * (c + 1)], mid_sb[:, uz, c, cut], ident_sb[:, :],
                                   start=False, stop=True, is_transpose=True, skip_group_check=True)
                tr.then_inc(o_filled, 1)

            def step(s, u, i):
                here, mid, late = active(s, 0), active(s, LAG_MID), active(s, LAG_OUT)
                for j in range(4):
                    if here:
                        transpose_item(s, u, i, j)
                    if j == 0 and active(s, LAG_MID + 1):
                        conv1_mid(s, u, 1, LAG_MID + 1)
                    if late:
                        out_tile(s, u, j)
                if late:
                    out_tile(s, u, 4)
                if here:
                    if active(s, LAG_MID + 1):
                        free = (h_ready[1], 2 * (s - LAG_MID - 1))
                    else:
                        free = (h_ready[0], 2 * (s - 1)) if active(s, 1) else None
                    for part in range(2):
                        conv1(0, s, part, xt_sb, xt_ready, 2, free)
                if mid:
                    mid_item(s, u, 0)
                    mid_item(s, u, 1)
                if late:
                    out_tile(s, u, 5)
                    out_tile(s, u, 6)
                if mid:
                    mid_item(s, u, 2)
                    conv1_mid(s, u, 0, LAG_MID)
                    mid_item(s, u, 3)

            pe.wait_ge(prep, PREP_STEPS)
            bias_matmuls()
            pe.wait_ge(prep, PREP_STEPS + 2 * LAYERS)
            run_steps(pe, step, TOTAL)

        @block.scalar
        def _(act):
            act.wait_ge(prep, 2)
            nc.scalar.activation(root_all, inv_all, ACT.Sqrt).then_inc(roots, 1)
            act.wait_ge(prep, PREP_STEPS + 2 * LAYERS)
            act.wait_ge(borders, LAYERS)

            def x_item(s, j):
                part, cp = divmod(j, 2)
                act.wait_ge(t0_filled, 4 * s + j + 1)
                if cp == 0 and active(s, 1):
                    act.wait_ge(c1_filled[0], 2 * (s - 1) + part + 1)
                a, b = span(part)
                pair = 2 * (j % 2)
                nc.scalar.copy(xt_sb[:, 2 * cp:2 * cp + 2, a:b], ps[:, pair:pair + 2, 0:b - a]).then_inc(xt_ready, 1)

            def h_part(n, v, uv, part, old):
                act.wait_ge(c1_filled[n], 2 * v + part + 1)
                if old:
                    act.wait_ge(taps_done[n], TAPS * (v - 2))
                a, b = span(part)
                r0 = 1 + ROWS * uv + a // W
                nc.scalar.activation(
                    h_sb[n][:, r0:r0 + (b - a) // W, 1:1 + W],
                    ps[:, 6 + part, 0:b - a].rearrange("p (r w) -> p r w", w=W),
                    ACT.Relu, bias=shift_c[:, BN * n:BN * n + 1]).then_inc(h_ready[n], 1)

            def h1_part(s, u, part, lag):
                h_part(1, s - lag, (u - lag) % UNITS, part, active(s, lag + 3))

            def mid_item(s, u, j):
                w = s - LAG_MID
                uw = (u - LAG_MID) % UNITS
                part, cp = divmod(j, 2)
                if cp == 0 and active(s, LAG_OUT):
                    act.wait_ge(o_filled, TILES * (w - 4) + PARTS[part][0] + PARTS[part][1])
                a, b = span(part)
                for k in range(2):
                    c = 2 * cp + k
                    act.wait_ge(mid_filled, 8 * w + 2 * j + k + 1)
                    nc.scalar.activation(mid_sb[:, uw, c, a:b], ps[:, 2 * (j % 2) + k, 0:b - a], ACT.Relu,
                                         bias=bias4_sb[:, 0, c:c + 1]).then_inc(mid_ready, 1)

            def add_bias(s, u, c):
                w = s - LAG_MID - 1
                uw = (u - LAG_MID - 1) % UNITS
                if c == 0:
                    act.wait_ge(c1_filled[1], 2 * w + 2)
                    act.wait_ge(mid_ready, 8 * w + 8)
                nc.scalar.activation(mid_sb[:, uw, c, :], mid_sb[:, uw, c, :], ACT.Identity,
                                     bias=bias4_sb[:, 1, c:c + 1]).then_inc(mid_biased, 1)

            def q_high(n, y, uy, slot_read):
                act.wait_ge(taps_done[n], TAPS * (y + 1))
                if slot_read is not None:
                    act.wait_ge(*slot_read)
                nc.scalar.copy(q_hi[n][:, uy % (n + 1), :], acc_sb[n][:, :, :].rearrange("p r w -> p (r w)")).then_inc(qh_ready[n], 1)

            def out_tile(s, u, t):
                z = s - LAG_OUT
                slot = u % 2
                act.wait_ge(o_filled, TILES * z + t + 1)
                for part in range(2):
                    if t == PARTS[part][0] and active(s, LAG_OUT + 2):
                        act.wait_ge(stored[slot][part], stores_before(s, u) * 16)
                nc.scalar.activation(out_sb[0:TILE, slot, t, :], ps[0:TILE, 4 + (u + t) % 2, :], ACT.Relu)\
                  .then_inc(o_ready, 1)

            def stores_before(s, u):
                if isinstance(s, int):
                    return (s - LAG_OUT) // 2
                return image[0] * (UNITS // 2) + (u - LAG_OUT) // 2

            image = [None]

            def step(s, u, i):
                image[0] = i
                here, mid, late = active(s, 0), active(s, LAG_MID), active(s, LAG_OUT)
                for j in range(4):
                    if here:
                        x_item(s, j)
                    if j == 0 and active(s, LAG_MID + 1):
                        h1_part(s, u, 1, LAG_MID + 1)
                    if late:
                        out_tile(s, u, j)
                    if j == 1 and active(s, 1 + LAG_DW0):
                        y = s - 1 - LAG_DW0
                        q_high(0, y, (u - 1 - LAG_DW0) % UNITS,
                               (mid_filled, 8 * y) if active(s, 2 + LAG_DW0) else None)
                    if j == 3 and active(s, 1 + LAG_DW1):
                        y = s - 1 - LAG_DW1
                        q_high(1, y, (u - 1 - LAG_DW1) % UNITS,
                               (o_filled, TILES * (y - 1)) if active(s, 3 + LAG_DW1) else None)
                if late:
                    out_tile(s, u, 4)
                if here:
                    for part in range(2):
                        h_part(0, s, u, part, active(s, 3))
                if active(s, LAG_MID + 1):
                    add_bias(s, u, 0)
                    add_bias(s, u, 1)
                if mid:
                    mid_item(s, u, 0)
                    mid_item(s, u, 1)
                if late:
                    out_tile(s, u, 5)
                    out_tile(s, u, 6)
                if mid:
                    mid_item(s, u, 2)
                    h1_part(s, u, 0, LAG_MID)
                    mid_item(s, u, 3)
                if active(s, LAG_MID + 1):
                    add_bias(s, u, 2)
                    add_bias(s, u, 3)

            run_steps(act, step, TOTAL)

        @block.vector
        def _(dve):
            done = [0]

            def then(ins):
                done[0] += 1
                ins.then_inc(prep, 1)
                dve.wait_ge(prep, done[0])

            dve.wait_ge(params_loaded, 16 * (6 + 2 * LAYERS))
            nc.vector.tensor_copy(gamma_all[:, 0:NBN], cols_sb[:, NBN:2 * NBN])
            nc.vector.tensor_scalar(var_all[:, 0:NBN], cols_sb[:, 0:NBN], EPS, None, ALU.add)
            then(nc.vector.tensor_scalar(var_all[:, NBN:], var_all[:, NBN:], EPS, None, ALU.add))
            then(nc.vector.reciprocal(inv_all, var_all))
            dve.wait_ge(roots, 1)
            then(nc.vector.reciprocal(var_all, root_all))
            then(nc.vector.tensor_tensor(var_all, var_all, inv_all, ALU.mult))
            then(nc.vector.tensor_tensor(root_all, root_all, var_all, ALU.add))
            then(nc.vector.scalar_tensor_tensor(out=inv_all, in0=root_all, scalar=0.5, in1=gamma_all,
                                                op0=ALU.mult, op1=ALU.mult))
            nc.vector.tensor_copy(scale_c[:, :], inv_all[:, 0:NBN])
            then(nc.vector.tensor_tensor(tmp_c[:, :], cols_sb[:, 4 * NBN:5 * NBN], cols_sb[:, 2 * NBN:3 * NBN],
                                         ALU.subtract))
            then(nc.vector.tensor_tensor(tmp_c[:, :], tmp_c[:, :], scale_c[:, :], ALU.mult))
            then(nc.vector.tensor_tensor(shift_c[:, :], tmp_c[:, :], cols_sb[:, 3 * NBN:4 * NBN], ALU.add))
            for l in range(LAYERS):
                b2, b3 = BN * l + 1, BN * l + 2
                raw = cols_sb[:, 5 * NBN + TAPS * l:5 * NBN + TAPS * (l + 1)]
                nc.vector.tensor_scalar(taps_sb[:, l, :], raw, scale_c[:, b2:b2 + 1], scale_c[:, b3:b3 + 1],
                                        ALU.mult, ALU.mult)
                nc.vector.tensor_scalar(beta_sb[:, l:l + 1], shift_c[:, b2:b2 + 1], scale_c[:, b3:b3 + 1],
                                        shift_c[:, b3:b3 + 1], ALU.mult, ALU.add)
                then(nc.vector.tensor_tensor(
                    w1_sb[:, l, :, :].rearrange("p c m -> p (c m)"), w1_f[:, HID * l:HID * (l + 1)],
                    scale_r[:, HID * l:HID * (l + 1)], ALU.mult))
            nc.vector.tensor_copy(tmp_c[:, 0:1], tmp_c[:, 1:2]).then_inc(prep, PREP_STEPS - done[0])
            done[0] = PREP_STEPS
            dve.wait_ge(prep, done[0])
            per = C // GROUPS
            for l in range(LAYERS):
                if l:
                    dve.wait_ge(bias_sums, l)
                src = w2_in[:, per * l:per * (l + 1)]
                for g in range(GROUPS):
                    last = nc.vector.tensor_scalar(w2_f[:, per * g:per * (g + 1)], src, masks_in[:, g:g + 1], None,
                                                   ALU.mult)
                last.then_inc(w2_placed, 1)
                dve.wait_ge(w2_placed, l + 1)
                r0 = LAYERS * HID + C * l
                nc.vector.tensor_tensor(w2_f, w2_f, scale_r[:, r0:r0 + C], ALU.mult).then_inc(prep, 1)
                dve.wait_ge(prep, PREP_STEPS + 2 * l + 1)
                nc.vector.tensor_copy(w2_hi[:, l, :], w2_f).then_inc(w2_split, 1)
                dve.wait_ge(w2_split, l + 1)
                nc.vector.tensor_tensor(w2_lo[:, l, :], w2_f, w2_hi[:, l, :].bitcast(F32), ALU.subtract)
                dve.wait_ge(bias_sums, l + 1)
                nc.vector.tensor_tensor(bias4_sb[:, l, :], ps[:, 4 + l, 0:CHUNKS],
                                        shift_c[:, BN * l + 3:BN * (l + 1)], ALU.add).then_inc(prep, 1)
                dve.wait_ge(prep, PREP_STEPS + 2 * l + 2)

            def tap(n, y, uy, k):
                dy, dx = divmod(k, 3)
                window = h_sb[n][:, ROWS * uy + dy:ROWS * uy + dy + ROWS, dx:dx + W]
                w = taps_sb[:, n, k:k + 1]
                if k == 0:
                    if not isinstance(y, int) or y > 0:
                        dve.wait_ge(ql_ready[n], y)
                    ins = nc.vector.tensor_scalar(acc_sb[n][:, :, :], window, w, None, ALU.mult)
                else:
                    dve.wait_ge(taps_done[n], TAPS * y + k)
                    ins = nc.vector.scalar_tensor_tensor(out=acc_sb[n][:, :, :], in0=window, scalar=w,
                                                         in1=acc_sb[n][:, :, :], op0=ALU.mult, op1=ALU.add)
                ins.then_inc(taps_done[n], 1)

            def q_low(n, y, uy):
                dve.wait_ge(qh_ready[n], y + 1)
                nc.vector.tensor_tensor(q_lo[n][:, uy % (n + 1), :], acc_sb[n][:, :, :].rearrange("p r w -> p (r w)"),
                                        q_hi[n][:, uy % (n + 1), :].bitcast(F32), ALU.subtract).then_inc(ql_ready[n], 1)

            def step(s, u, i):
                on = [active(s, LAG_DW0), active(s, LAG_DW1)]
                ys = [s - LAG_DW0, s - LAG_DW1]
                us = [(u - LAG_DW0) % UNITS, (u - LAG_DW1) % UNITS]
                for n in range(LAYERS):
                    if on[n]:
                        more = 1 if us[n] < UNITS - 1 else 0
                        dve.wait_ge(h_ready[n], 2 * (ys[n] + 1) + more)
                for k in range(TAPS):
                    for n in range(LAYERS):
                        if on[n]:
                            tap(n, ys[n], us[n], k)
                for n in range(LAYERS):
                    if on[n]:
                        q_low(n, ys[n], us[n])

            run_steps(dve, step, TOTAL)


_BNS = [(1, "b1"), (2, "dw_b"), (3, None), (4, "b2")]


def _hidden(v):
    return v.reshape(HID // GROUPS, GROUPS, *v.shape[1:]).swapaxes(0, 1).reshape(v.shape)


def _columns(inputs, what):
    cols = []
    for l in range(LAYERS):
        for n, conv_bias in _BNS:
            name = what or conv_bias
            if what:
                v = np.asarray(inputs[f"L{l}_conv_bn{n}_{what}"])
            elif conv_bias:
                v = np.asarray(inputs[f"L{l}_conv_{conv_bias}"])
            else:
                v = np.zeros(HID, np.float32)
            if n in (2, 3):
                v = _hidden(v)
            cols += list(v.reshape(-1, P))
    return cols


def kernel(**inputs):
    import concourse.bacc as bacc
    from concourse.bass_utils import run_bass_kernel_spmd

    cols = [c for what in ("v", "g", "m", "b", None) for c in _columns(inputs, what)]
    for l in range(LAYERS):
        cols += list(_hidden(np.asarray(inputs[f"L{l}_conv_dw_w"]).reshape(TAPS, HID).T).T)
    rows = {w: np.concatenate([np.asarray(inputs[f"L{l}_conv_bn{n}_{w}"]) for n in (1, 4) for l in range(LAYERS)])
            for w in "gv"}
    w2 = np.concatenate([_hidden(np.asarray(inputs[f"L{l}_conv_w2"]).reshape(HID, C // GROUPS))
                         for l in range(LAYERS)], axis=1)
    group = _hidden(np.arange(HID) // (HID // GROUPS))
    arrays = {
        "x": np.ascontiguousarray(inputs["x"]),
        "cols": np.ascontiguousarray(np.stack(cols, axis=1)),
        "gamma_row": rows["g"],
        "var_row": rows["v"],
        "w1": np.stack([np.asarray(inputs[f"L{l}_conv_w1"]) for l in range(LAYERS)]),
        "w2": np.ascontiguousarray(w2),
        "masks": (group[:, None] == np.arange(GROUPS)).astype(np.float32),
        "ident": np.eye(P, dtype=np.float32),
    }
    nc = bacc.Bacc("TRN2", target_bir_lowering=False, num_devices=1)
    aps = [nc.dram_tensor(n, a.shape, mybir.dt.from_np(a.dtype), kind="ExternalInput").ap() for n, a in arrays.items()]
    out = nc.dram_tensor("out", (IMAGES, H, W, C), F32, kind="ExternalOutput").ap()
    conv_stack_kernel(nc, *aps, out)
    r = run_bass_kernel_spmd(nc, [arrays], core_ids=[0])
    return r.results[0]["out"]
```

```python
from contextlib import ExitStack

import numpy as np

import concourse.bass as bass
from concourse import mybir

ALU = mybir.AluOpType
ACT = mybir.ActivationFunctionType
F32 = mybir.dt.float32
F32R = mybir.dt.float32r

LAYERS = 2
IMAGES, H, W, C = 32, 56, 56, 512
GROUPS = 8
HID = C // 4
EPS = 1e-3
P = 128

UNITS = 4
ROWS = H // UNITS
TILE = 2 * W
TILES = ROWS // 2
UPIX = ROWS * W
PARTS = ((0, 4), (4, 3))
CHUNKS = C // P
PW, PH = W + 2, H + 2
TOTAL = IMAGES * UNITS

Q_LOW_AT = (2, 3)
LAG_DW0, LAG_MID, LAG_DW1, LAG_OUT = 1, 2, 4, 6
PEELED = -(-LAG_OUT // UNITS)

HALVES = 2
HROWS = HID // HALVES
HALF_C = C // HALVES
BN = 3 + CHUNKS + 2
NBN = LAYERS * BN
TAPS = 9
COLS = 5 * NBN + LAYERS * TAPS
ROWLEN = LAYERS * (HID + C)


def conv_stack_kernel(nc, x, cols, gamma_row, var_row, w1, w2, masks, ident, out):
    x_v = x.rearrange("n (u t r) w c -> (n u) (r w) t c", u=UNITS, t=TILES)
    out_v = out.rearrange("n (u t r) w c -> (n u) (r w) t c", u=UNITS, t=TILES)

    with ExitStack() as ctx:
        def sb(name, shape, dt=F32):
            return ctx.enter_context(nc.sbuf_tensor(name, shape, dt))

        def sem(name):
            return ctx.enter_context(nc.semaphore(name))

        x_sb = sb("x_sb", [TILE, UNITS, TILES, C])
        xt_sb = sb("xt_sb", [P, CHUNKS, UPIX])
        h_sb = [sb(f"h{n}_sb", [P, PH, PW]) for n in range(LAYERS)]
        acc_sb = [sb(f"acc{n}_sb", [P, 2, ROWS, W]) for n in range(LAYERS)]
        q_hi = [sb(f"q{n}_hi", [P, UPIX], F32R) for n in range(LAYERS)]
        stack = [sb(f"stack{n}", [P, n + 1, HALVES, UPIX], F32R) for n in range(LAYERS)]
        mid_sb = sb("mid_sb", [P, UNITS, CHUNKS, UPIX])
        out_sb = sb("out_sb", [P, 2, TILES, C])
        ident_sb = sb("ident_sb", [P, P])
        cols_sb = sb("cols_sb", [P, COLS])
        w1_sb = sb("w1_sb", [P, LAYERS, CHUNKS, HID // CHUNKS])
        w2_hi = sb("w2_hi", [P, LAYERS, C], F32R)
        w2_lo = sb("w2_lo", [P, LAYERS, C], F32R)
        scale_c = sb("scale_c", [P, NBN])
        shift_c = sb("shift_c", [P, NBN])
        tmp_c = sb("tmp_c", [P, NBN])
        taps_sb = sb("taps_sb", [P, LAYERS, TAPS])
        beta_sb = sb("beta_sb", [P, LAYERS])
        bias4_sb = sb("bias4_sb", [P, LAYERS, CHUNKS])
        scratch = out_sb[:, :, :, :].rearrange("p s t c -> p (s t c)")
        place = [0]

        def carve(n):
            place[0] += n
            return scratch[:, place[0] - n:place[0]]

        var_all, gamma_all, root_all, inv_all = (carve(NBN + ROWLEN) for _ in range(4))
        w2_in, masks_in = carve(LAYERS * HALVES * C // GROUPS), carve(GROUPS // HALVES)
        w2_f = carve(C)
        w1_f = carve(LAYERS * HID)
        scale_r = inv_all[:, NBN:]

        ps = ctx.enter_context(nc.psum_tensor("ps", [P, 8, 512], F32))

        x_loaded = [[sem(f"x_loaded_{u}_{part}") for part in range(2)] for u in range(UNITS)]
        params_loaded = sem("params_loaded")
        prep = sem("prep")
        roots = sem("roots")
        bias_sums = sem("bias_sums")
        w2_placed = sem("w2_placed")
        w2_split = sem("w2_split")
        borders = sem("borders")
        blocks = sem("blocks")
        t0_filled = sem("t0_filled")
        xt_ready = sem("xt_ready")
        c1_filled = [sem(f"c1_{n}_filled") for n in range(LAYERS)]
        h_ready = [sem(f"h{n}_ready") for n in range(LAYERS)]
        tap0_done = sem("tap0_done")
        taps_done = [sem(f"taps{n}_done") for n in range(LAYERS)]
        qh_ready = [sem(f"q{n}_hi_ready") for n in range(LAYERS)]
        ql_ready = [sem(f"q{n}_lo_ready") for n in range(LAYERS)]
        stacked = [[sem(f"stacked{n}_{k}") for k in range(n + 1)] for n in range(LAYERS)]
        mid_filled = sem("mid_filled")
        mid_ready = sem("mid_ready")
        mid_biased = sem("mid_biased")
        o_filled = sem("o_filled")
        o_ready = sem("o_ready")
        stored = [[sem(f"stored_{s}_{part}") for part in range(2)] for s in range(2)]

        STACKED = 16 * 2 * HALVES

        def stacked_wait(eng, n, v, u):
            if n == 0:
                eng.wait_ge(stacked[0][0], STACKED * (v + 1))
            else:
                eng.wait_ge(stacked[1][u % 2], STACKED * (v // 2 + 1))

        PREP_STEPS = 64

        def span(part):
            first, n = PARTS[part]
            return first * TILE, (first + n) * TILE

        def active(s, lag):
            return not isinstance(s, int) or 0 <= s - lag < TOTAL

        def run_steps(eng, step, last):
            for s in range(PEELED * UNITS):
                step(s, s % UNITS, s // UNITS)
            with_tail = (last - TOTAL) // UNITS if last < TOTAL else 0
            end = IMAGES + with_tail
            with eng.Fori(PEELED, end) as i:
                for u in range(UNITS):
                    step(UNITS * i + u, u, i)
            for s in range(end * UNITS, TOTAL + LAG_OUT):
                step(s, s % UNITS, s // UNITS)

        block = ctx.enter_context(nc.Block())

        @block.sync
        def _(sp):
            def load(v, u):
                for part, (t, n) in enumerate(PARTS):
                    sp.dma_start(x_sb[:, u, t:t + n, :], x_v[v][:, t:t + n, :]).then_inc(x_loaded[u][part], 16)

            sp.dma_start(ident_sb[:, :], ident).then_inc(params_loaded, 16)
            load(0, 0)
            sp.dma_start(cols_sb[:, :], cols).then_inc(params_loaded, 16)
            sp.dma_start(var_all[:, NBN:], var_row.partition_broadcast(P)).then_inc(params_loaded, 16)
            sp.dma_start(gamma_all[:, NBN:], gamma_row.partition_broadcast(P)).then_inc(params_loaded, 16)
            sp.dma_start(w2_in, w2).then_inc(params_loaded, 16)
            sp.dma_start(masks_in, masks).then_inc(params_loaded, 16)
            sp.wait_ge(blocks, 1)
            half = P // 2
            w1_f4 = w1_f.rearrange("p (l c m) -> p l c m", l=LAYERS, c=CHUNKS)
            for l in range(LAYERS):
                for t in range(2):
                    src = w1[l].rearrange("(c t) k d -> t k c d", t=2)[t]
                    sp.dma_start(w1_f4[half * t:half * (t + 1), l, :, 16 * t:16 * (t + 1)], src)\
                      .then_inc(params_loaded, 16)
            load(1, 1)

            def store(z, s, u, part):
                sp.wait_ge(o_ready, TILES * z + PARTS[part][0] + PARTS[part][1])
                t, n = PARTS[part]
                sp.dma_start(out_v[z][:, t:t + n, :], out_sb[0:TILE, s, t:t + n, :]).then_inc(stored[s][part], 16)

            def stack_halves(n, y, uy):
                slot = uy % (n + 1)
                low = acc_sb[n][:, uy % 2, :, :].rearrange("p r w -> p (r w)")
                for k, (ready, src) in enumerate(((qh_ready[n], q_hi[n][:, :].bitcast(F32)), (ql_ready[n], low))):
                    sp.wait_ge(ready, y + 1)
                    for h in range(HALVES):
                        sp.dma_start(stack[n][HROWS * k:HROWS * (k + 1), slot, h, :].bitcast(F32), src[h::HALVES, :])\
                          .then_inc(stacked[n][slot], 16)

            def step(s, u, i):
                if active(s, LAG_OUT):
                    store(s - LAG_OUT, u % 2, u, 0)
                    store(s - LAG_OUT, u % 2, u, 1)
                if active(s, LAG_DW0):
                    stack_halves(0, s - LAG_DW0, (u - LAG_DW0) % UNITS)
                if active(s, LAG_DW1):
                    stack_halves(1, s - LAG_DW1, (u - LAG_DW1) % UNITS)
                if active(s, -2):
                    if active(s, LAG_MID):
                        sp.wait_ge(mid_filled, 8 * (s - LAG_MID + 1))
                    load(s + 2, (u + 2) % UNITS)

            run_steps(sp, step, TOTAL - UNITS)
            for s in range(2):
                for part in range(2):
                    sp.wait_ge(stored[s][part], 16 * (TOTAL // 2))

        @block.gpsimd
        def _(pool):
            w1_zero = w1_f
            nc.gpsimd.memset(w1_zero, 0.0).then_inc(blocks, 1)
            for n in range(LAYERS):
                nc.gpsimd.memset(h_sb[n][:, :, :], 0.0).then_inc(borders, 1)

        @block.tensor
        def _(pe):
            pe.wait_ge(params_loaded, 16 * (6 + 2 * LAYERS))

            def bias_matmuls():
                for l in range(LAYERS):
                    pe.wait_ge(prep, PREP_STEPS + 2 * l + 1)
                    for c in range(CHUNKS):
                        bank = 4 + HALVES * l + P * c // HALF_C
                        h = HROWS * (P * c // HALF_C)
                        mm = pe.matmul(ps[:, bank, c:c + 1], w2_f[h:h + HROWS, P * c:P * (c + 1)],
                                       beta_sb[h:h + HROWS, l:l + 1],
                                       start=True, stop=True, skip_group_check=True)
                    mm.then_inc(bias_sums, 1)

            def transpose_item(s, u, i, j):
                part, cp = divmod(j, 2)
                if cp == 0:
                    pe.wait_ge(x_loaded[u][part], 16 * (i + 1))
                if j >= 2:
                    pe.wait_ge(xt_ready, 4 * s + j - 1)
                elif active(s, LAG_MID + 1):
                    pe.wait_ge(mid_ready, 8 * (s - LAG_MID - 1) + 2 * (j + 3))
                elif active(s, 1):
                    pe.wait_ge(xt_ready, 4 * (s - 1) + j + 3)
                first, n = PARTS[part]
                for k in range(2):
                    c = 2 * cp + k
                    for t in range(n):
                        tr = pe.transpose(ps[:, 2 * (j % 2) + k, TILE * t:TILE * (t + 1)],
                                          x_sb[:, u, first + t, P * c:P * (c + 1)], ident_sb[0:TILE, 0:TILE])
                tr.then_inc(t0_filled, 1)

            def conv1(n, v, part, src, ready, per_part, bank_free):
                pe.wait_ge(ready, 2 * per_part * v + per_part * (part + 1))
                if bank_free is not None:
                    pe.wait_ge(bank_free[0], bank_free[1] + part + 1)
                a, b = span(part)
                for c in range(CHUNKS):
                    mm = pe.matmul(ps[32 * c:32 * (c + 1), 6 + part, 0:b - a], w1_sb[:, n, c, :],
                                   src[:, c, a:b], start=True, stop=True)
                mm.then_inc(c1_filled[n], 1)

            def conv1_mid(s, u, part, lag):
                w = s - lag
                if active(s, lag - LAG_MID):
                    free = (h_ready[0], 2 * (s - lag + LAG_MID))
                else:
                    free = (h_ready[1], 2 * (w - 1))
                conv1(1, w, part, mid_sb[:, (u - lag) % UNITS, :, :], mid_ready, 4, free)

            def mid_item(s, u, j):
                w = s - LAG_MID
                uw = (u - LAG_MID) % UNITS
                part, cp = divmod(j, 2)
                if j == 0:
                    stacked_wait(pe, 0, w, uw)
                if j >= 2:
                    pe.wait_ge(mid_ready, 8 * w + 2 * (j - 1))
                elif active(s, 0):
                    pe.wait_ge(xt_ready, 4 * s + j + 3)
                else:
                    pe.wait_ge(mid_ready, 8 * (w - 1) + 2 * (j + 3))
                a, b = span(part)
                first, n = PARTS[part]
                for k in range(2):
                    c = 2 * cp + k
                    bank = 2 * (j % 2) + k
                    for wt in (w2_hi, w2_lo):
                        pe.matmul(ps[:, bank, 0:b - a], wt[:, 0, P * c:P * (c + 1)],
                                  stack[0][:, 0, P * c // HALF_C, a:b], start=(wt is w2_hi), stop=(wt is w2_lo))
                    for t in range(n):
                        tr = pe.matmul(ps[:, bank, TILE * t:TILE * (t + 1)],
                                       x_sb[:, uw, first + t, P * c:P * (c + 1)], ident_sb[0:TILE, 0:TILE],
                                       start=False, stop=True, is_transpose=True, skip_group_check=True)
                    tr.then_inc(mid_filled, 1)

            def out_tile(s, u, t):
                z = s - LAG_OUT
                uz = (u - LAG_OUT) % UNITS
                bank = 4 + (u + t) % 2
                if t == 0:
                    stacked_wait(pe, 1, z, uz)
                    pe.wait_ge(mid_biased, 4 * (z + 1))
                if not isinstance(z, int) or z > 0 or t >= 2:
                    pe.wait_ge(o_ready, TILES * z + t - 1)
                cut = slice(TILE * t, TILE * (t + 1))
                for h in range(HALVES):
                    cols_h = slice(HALF_C * h, HALF_C * (h + 1))
                    for wt in (w2_hi, w2_lo):
                        pe.matmul(ps[0:TILE, bank, cols_h], stack[1][:, uz % 2, h, cut], wt[:, 1, cols_h],
                                  start=(h == 0 and wt is w2_hi), stop=(wt is w2_lo), skip_group_check=True)
                for c in range(CHUNKS):
                    tr = pe.matmul(ps[0:TILE, bank, P * c:P * (c + 1)], mid_sb[:, uz, c, cut], ident_sb[:, :],
                                   start=False, stop=True, is_transpose=True, skip_group_check=True)
                tr.then_inc(o_filled, 1)

            def step(s, u, i):
                here, mid, late = active(s, 0), active(s, LAG_MID), active(s, LAG_OUT)
                for j in range(4):
                    if here:
                        transpose_item(s, u, i, j)
                    if j == 0 and active(s, LAG_MID + 1):
                        conv1_mid(s, u, 1, LAG_MID + 1)
                    if late:
                        out_tile(s, u, j)
                if late:
                    out_tile(s, u, 4)
                if here:
                    if active(s, LAG_MID + 1):
                        free = (h_ready[1], 2 * (s - LAG_MID - 1))
                    else:
                        free = (h_ready[0], 2 * (s - 1)) if active(s, 1) else None
                    for part in range(2):
                        conv1(0, s, part, xt_sb, xt_ready, 2, free)
                if mid:
                    mid_item(s, u, 0)
                    mid_item(s, u, 1)
                if late:
                    out_tile(s, u, 5)
                    out_tile(s, u, 6)
                if mid:
                    mid_item(s, u, 2)
                    conv1_mid(s, u, 0, LAG_MID)
                    mid_item(s, u, 3)

            pe.wait_ge(prep, PREP_STEPS)
            bias_matmuls()
            pe.wait_ge(prep, PREP_STEPS + 2 * LAYERS)
            run_steps(pe, step, TOTAL)

        @block.scalar
        def _(act):
            act.wait_ge(prep, 2)
            nc.scalar.activation(root_all, inv_all, ACT.Sqrt).then_inc(roots, 1)
            act.wait_ge(prep, PREP_STEPS + 2 * LAYERS)
            act.wait_ge(borders, LAYERS)

            def x_item(s, j):
                part, cp = divmod(j, 2)
                act.wait_ge(t0_filled, 4 * s + j + 1)
                if cp == 0 and active(s, 1):
                    act.wait_ge(c1_filled[0], 2 * (s - 1) + part + 1)
                a, b = span(part)
                pair = 2 * (j % 2)
                nc.scalar.copy(xt_sb[:, 2 * cp:2 * cp + 2, a:b], ps[:, pair:pair + 2, 0:b - a]).then_inc(xt_ready, 1)

            def h_part(n, v, uv, part, old):
                act.wait_ge(c1_filled[n], 2 * v + part + 1)
                if old:
                    act.wait_ge(taps_done[n], (TAPS - 1 + n) * (v - 2))
                a, b = span(part)
                r0 = 1 + ROWS * uv + a // W
                nc.scalar.activation(
                    h_sb[n][:, r0:r0 + (b - a) // W, 1:1 + W],
                    ps[:, 6 + part, 0:b - a].rearrange("p (r w) -> p r w", w=W),
                    ACT.Relu, bias=shift_c[:, BN * n:BN * n + 1]).then_inc(h_ready[n], 1)

            def h1_part(s, u, part, lag):
                h_part(1, s - lag, (u - lag) % UNITS, part, active(s, lag + 3))

            def mid_item(s, u, j):
                w = s - LAG_MID
                uw = (u - LAG_MID) % UNITS
                part, cp = divmod(j, 2)
                if cp == 0 and active(s, LAG_OUT):
                    act.wait_ge(o_filled, TILES * (w - 4) + PARTS[part][0] + PARTS[part][1])
                a, b = span(part)
                for k in range(2):
                    c = 2 * cp + k
                    act.wait_ge(mid_filled, 8 * w + 2 * j + k + 1)
                    nc.scalar.activation(mid_sb[:, uw, c, a:b], ps[:, 2 * (j % 2) + k, 0:b - a], ACT.Relu,
                                         bias=bias4_sb[:, 0, c:c + 1]).then_inc(mid_ready, 1)

            def add_bias(s, u, c):
                w = s - LAG_MID - 1
                uw = (u - LAG_MID - 1) % UNITS
                if c == 0:
                    act.wait_ge(c1_filled[1], 2 * w + 2)
                    act.wait_ge(mid_ready, 8 * w + 8)
                nc.scalar.activation(mid_sb[:, uw, c, :], mid_sb[:, uw, c, :], ACT.Identity,
                                     bias=bias4_sb[:, 1, c:c + 1]).then_inc(mid_biased, 1)

            def q_high(n, y, uy, units_before):
                act.wait_ge(taps_done[n], (TAPS - 1 + n) * (y + 1))
                if n == 0 and units_before >= 1:
                    act.wait_ge(mid_filled, 8 * y)
                if n == 1 and units_before >= 1:
                    stacked_wait(act, 1, y - 1, uy - 1)
                if n == 1 and units_before >= 2:
                    act.wait_ge(o_filled, TILES * (y - 1))
                nc.scalar.copy(q_hi[n][:, :], acc_sb[n][:, uy % 2, :, :].rearrange("p r w -> p (r w)"))\
                  .then_inc(qh_ready[n], 1)

            def tap0(y, uy, old):
                act.wait_ge(h_ready[0], 2 * (y + 1))
                if old:
                    stacked_wait(act, 0, y - 2, uy)
                nc.scalar.activation(acc_sb[0][:, uy % 2, :, :], h_sb[0][:, ROWS * uy:ROWS * (uy + 1), 0:W], ACT.Copy,
                                     scale=taps_sb[:, 0, 0:1]).then_inc(tap0_done, 1)

            def out_tile(s, u, t):
                z = s - LAG_OUT
                slot = u % 2
                act.wait_ge(o_filled, TILES * z + t + 1)
                for part in range(2):
                    if t == PARTS[part][0] and active(s, LAG_OUT + 2):
                        act.wait_ge(stored[slot][part], stores_before(s, u) * 16)
                nc.scalar.activation(out_sb[0:TILE, slot, t, :], ps[0:TILE, 4 + (u + t) % 2, :], ACT.Relu)\
                  .then_inc(o_ready, 1)

            def stores_before(s, u):
                if isinstance(s, int):
                    return (s - LAG_OUT) // 2
                return image[0] * (UNITS // 2) + (u - LAG_OUT) // 2

            image = [None]

            def step(s, u, i):
                image[0] = i
                here, mid, late = active(s, 0), active(s, LAG_MID), active(s, LAG_OUT)
                for j in range(4):
                    if here:
                        x_item(s, j)
                    if j == 0 and active(s, LAG_MID + 1):
                        h1_part(s, u, 1, LAG_MID + 1)
                    if late:
                        out_tile(s, u, j)
                    if j == 0 and active(s, 1 + LAG_DW0):
                        y = s - 1 - LAG_DW0
                        q_high(0, y, (u - 1 - LAG_DW0) % UNITS, 2 if active(s, 3 + LAG_DW0) else y)
                    if j == 1 and active(s, 1 + LAG_DW1):
                        y = s - 1 - LAG_DW1
                        q_high(1, y, (u - 1 - LAG_DW1) % UNITS, 2 if active(s, 3 + LAG_DW1) else y)
                if late:
                    out_tile(s, u, 4)
                if here:
                    for part in range(2):
                        h_part(0, s, u, part, active(s, 3))
                    tap0(s, u, active(s, 2))
                if active(s, LAG_MID + 1):
                    add_bias(s, u, 0)
                    add_bias(s, u, 1)
                if mid:
                    mid_item(s, u, 0)
                    mid_item(s, u, 1)
                if late:
                    out_tile(s, u, 5)
                    out_tile(s, u, 6)
                if mid:
                    mid_item(s, u, 2)
                    h1_part(s, u, 0, LAG_MID)
                    mid_item(s, u, 3)
                if active(s, LAG_MID + 1):
                    add_bias(s, u, 2)
                    add_bias(s, u, 3)

            run_steps(act, step, TOTAL)

        @block.vector
        def _(dve):
            done = [0]

            def then(ins):
                done[0] += 1
                ins.then_inc(prep, 1)
                dve.wait_ge(prep, done[0])

            dve.wait_ge(params_loaded, 16 * (6 + 2 * LAYERS))
            nc.vector.tensor_copy(gamma_all[:, 0:NBN], cols_sb[:, NBN:2 * NBN])
            nc.vector.tensor_scalar(var_all[:, 0:NBN], cols_sb[:, 0:NBN], EPS, None, ALU.add)
            then(nc.vector.tensor_scalar(var_all[:, NBN:], var_all[:, NBN:], EPS, None, ALU.add))
            then(nc.vector.reciprocal(inv_all, var_all))
            dve.wait_ge(roots, 1)
            then(nc.vector.reciprocal(var_all, root_all))
            then(nc.vector.tensor_tensor(var_all, var_all, inv_all, ALU.mult))
            then(nc.vector.tensor_tensor(root_all, root_all, var_all, ALU.add))
            then(nc.vector.scalar_tensor_tensor(out=inv_all, in0=root_all, scalar=0.5, in1=gamma_all,
                                                op0=ALU.mult, op1=ALU.mult))
            nc.vector.tensor_copy(scale_c[:, :], inv_all[:, 0:NBN])
            then(nc.vector.tensor_tensor(tmp_c[:, :], cols_sb[:, 4 * NBN:5 * NBN], cols_sb[:, 2 * NBN:3 * NBN],
                                         ALU.subtract))
            then(nc.vector.tensor_tensor(tmp_c[:, :], tmp_c[:, :], scale_c[:, :], ALU.mult))
            then(nc.vector.tensor_tensor(shift_c[:, :], tmp_c[:, :], cols_sb[:, 3 * NBN:4 * NBN], ALU.add))
            for l in range(LAYERS):
                b2, b3 = BN * l + 1, BN * l + 2
                s2, s3 = BN * l + BN - 2, BN * l + BN - 1
                raw = cols_sb[:, 5 * NBN + TAPS * l:5 * NBN + TAPS * (l + 1)]
                nc.vector.tensor_scalar(taps_sb[:, l, :], raw, scale_c[:, b2:b2 + 1], scale_c[:, b3:b3 + 1],
                                        ALU.mult, ALU.mult)
                nc.vector.tensor_scalar(beta_sb[:, l:l + 1], shift_c[:, s2:s2 + 1], scale_c[:, s3:s3 + 1],
                                        shift_c[:, s3:s3 + 1], ALU.mult, ALU.add)
                then(nc.vector.tensor_tensor(
                    w1_sb[:, l, :, :].rearrange("p c m -> p (c m)"), w1_f[:, HID * l:HID * (l + 1)],
                    scale_r[:, HID * l:HID * (l + 1)], ALU.mult))
            nc.vector.tensor_copy(tmp_c[:, 0:1], tmp_c[:, 1:2]).then_inc(prep, PREP_STEPS - done[0])
            done[0] = PREP_STEPS
            dve.wait_ge(prep, done[0])
            per = C // GROUPS
            for l in range(LAYERS):
                if l:
                    dve.wait_ge(bias_sums, l)
                for g in range(GROUPS):
                    h, k = divmod(g, GROUPS // HALVES)
                    src = w2_in[:, per * (HALVES * l + h):per * (HALVES * l + h + 1)]
                    last = nc.vector.tensor_scalar(w2_f[:, per * g:per * (g + 1)], src, masks_in[:, k:k + 1], None,
                                                   ALU.mult)
                last.then_inc(w2_placed, 1)
                dve.wait_ge(w2_placed, l + 1)
                r0 = LAYERS * HID + C * l
                nc.vector.tensor_tensor(w2_f, w2_f, scale_r[:, r0:r0 + C], ALU.mult).then_inc(prep, 1)
                dve.wait_ge(prep, PREP_STEPS + 2 * l + 1)
                nc.vector.tensor_copy(w2_hi[:, l, :], w2_f).then_inc(w2_split, 1)
                dve.wait_ge(w2_split, l + 1)
                nc.vector.tensor_tensor(w2_lo[:, l, :], w2_f, w2_hi[:, l, :].bitcast(F32), ALU.subtract)
                dve.wait_ge(bias_sums, l + 1)
                for h in range(HALVES):
                    c0, c1 = CHUNKS // HALVES * h, CHUNKS // HALVES * (h + 1)
                    last = nc.vector.tensor_tensor(
                        bias4_sb[:, l, c0:c1], ps[:, 4 + HALVES * l + h, c0:c1],
                        shift_c[:, BN * l + 3 + c0:BN * l + 3 + c1], ALU.add)
                last.then_inc(prep, 1)
                dve.wait_ge(prep, PREP_STEPS + 2 * l + 2)

            def tap(n, y, uy, k, old):
                dy, dx = divmod(k, 3)
                window = h_sb[n][:, ROWS * uy + dy:ROWS * uy + dy + ROWS, dx:dx + W]
                w = taps_sb[:, n, k:k + 1]
                total = acc_sb[n][:, uy % 2, :, :]
                if k == 0:
                    if old:
                        stacked_wait(dve, n, y - 2, uy)
                    ins = nc.vector.tensor_scalar(total, window, w, None, ALU.mult)
                else:
                    if n == 0 and k == 1:
                        dve.wait_ge(tap0_done, y + 1)
                    else:
                        dve.wait_ge(taps_done[n], (TAPS - 1 + n) * y + k - 1 + n)
                    ins = nc.vector.scalar_tensor_tensor(out=total, in0=window, scalar=w, in1=total,
                                                         op0=ALU.mult, op1=ALU.add)
                ins.then_inc(taps_done[n], 1)

            def q_low(n, y, uy):
                dve.wait_ge(qh_ready[n], y + 1)
                total = acc_sb[n][:, uy % 2, :, :].rearrange("p r w -> p (r w)")
                nc.vector.tensor_tensor(total.bitcast(F32R), total, q_hi[n][:, :].bitcast(F32), ALU.subtract)\
                  .then_inc(ql_ready[n], 1)

            def step(s, u, i):
                on = [active(s, LAG_DW0), active(s, LAG_DW1)]
                ys = [s - LAG_DW0, s - LAG_DW1]
                us = [(u - LAG_DW0) % UNITS, (u - LAG_DW1) % UNITS]
                below = [1 if v < UNITS - 1 else 0 for v in us]
                for k in range(TAPS):
                    for n in range(LAYERS):
                        if on[n] and k == 0:
                            dve.wait_ge(h_ready[n], 2 * (ys[n] + 1))
                        if on[n] and k == TAPS - 3:
                            dve.wait_ge(h_ready[n], 2 * (ys[n] + 1) + below[n])
                        if on[n] and not (n == 0 and k == 0):
                            tap(n, ys[n], us[n], k, active(s, (LAG_DW0, LAG_DW1)[n] + 2))
                        if k == Q_LOW_AT[n] and active(s, (LAG_DW0, LAG_DW1)[n] + 1):
                            q_low(n, ys[n] - 1, (us[n] - 1) % UNITS)

            run_steps(dve, step, TOTAL)


_BNS = [(1, "b1"), (2, "dw_b"), (3, None), (4, "b2")]


PER_GROUP = HID // GROUPS


def _halves(v):
    return v.reshape(GROUPS, HALVES, PER_GROUP // HALVES, *v.shape[1:]).swapaxes(1, 2).reshape(v.shape)


def _hidden(v):
    return v.reshape(HALVES, PER_GROUP // HALVES, GROUPS, *v.shape[1:]).swapaxes(0, 2).reshape(v.shape)


def _stacked(v):
    return v.reshape(HALVES, PER_GROUP // HALVES, GROUPS, *v.shape[1:]).swapaxes(1, 2).reshape(v.shape)


def _columns(inputs, what):
    cols = []
    for l in range(LAYERS):
        v = {}
        for n, conv_bias in _BNS:
            name = f"bn{n}_{what}" if what else conv_bias
            v[n] = np.asarray(inputs[f"L{l}_conv_{name}"]) if name else np.zeros(HID, np.float32)
        cols += [_halves(v[1]), _hidden(v[2]), _hidden(v[3]), *v[4].reshape(-1, P), _stacked(v[2]), _stacked(v[3])]
    return cols


def kernel(**inputs):
    import concourse.bacc as bacc
    from concourse.bass_utils import run_bass_kernel_spmd

    cols = [c for what in ("v", "g", "m", "b", None) for c in _columns(inputs, what)]
    for l in range(LAYERS):
        cols += list(_hidden(np.asarray(inputs[f"L{l}_conv_dw_w"]).reshape(TAPS, HID).T).T)
    rows = {w: np.concatenate([_halves(np.asarray(inputs[f"L{l}_conv_bn1_{w}"])) for l in range(LAYERS)]
                              + [np.asarray(inputs[f"L{l}_conv_bn4_{w}"]) for l in range(LAYERS)])
            for w in "gv"}
    w1 = np.stack([np.asarray(inputs[f"L{l}_conv_w1"]) for l in range(LAYERS)])
    w1 = w1.reshape(LAYERS, GROUPS, C // GROUPS, HALVES, -1).swapaxes(3, 4).reshape(w1.shape)
    w2 = [_stacked(np.asarray(inputs[f"L{l}_conv_w2"]).reshape(HID, C // GROUPS))[HROWS * h:HROWS * (h + 1)]
          for l in range(LAYERS) for h in range(HALVES)]
    w2 = np.tile(np.concatenate(w2, axis=1), (2, 1))
    group = _stacked(np.arange(HID) // PER_GROUP) % (GROUPS // HALVES)
    arrays = {
        "x": np.ascontiguousarray(inputs["x"]),
        "cols": np.ascontiguousarray(np.stack(cols, axis=1)),
        "gamma_row": rows["g"],
        "var_row": rows["v"],
        "w1": np.ascontiguousarray(w1),
        "w2": np.ascontiguousarray(w2),
        "masks": (group[:, None] == np.arange(GROUPS // HALVES)).astype(np.float32),
        "ident": np.eye(P, dtype=np.float32),
    }
    nc = bacc.Bacc("TRN2", target_bir_lowering=False, num_devices=1, dynamic_dma_scratch_size=1024)
    aps = [nc.dram_tensor(n, a.shape, mybir.dt.from_np(a.dtype), kind="ExternalInput").ap() for n, a in arrays.items()]
    out = nc.dram_tensor("out", (IMAGES, H, W, C), F32, kind="ExternalOutput").ap()
    conv_stack_kernel(nc, *aps, out)
    r = run_bass_kernel_spmd(nc, [arrays], core_ids=[0])
    return r.results[0]["out"]
```

```python
from contextlib import ExitStack

import numpy as np

import concourse.bass as bass
from concourse import mybir

ALU = mybir.AluOpType
ACT = mybir.ActivationFunctionType
F32 = mybir.dt.float32
F32R = mybir.dt.float32r

LAYERS = 2
IMAGES, H, W, C = 32, 56, 56, 512
GROUPS = 8
HID = C // 4
EPS = 1e-3
P = 128

UNITS = 4
ROWS = H // UNITS
TILE = 2 * W
TILES = ROWS // 2
UPIX = ROWS * W
PARTS = ((0, 4), (4, 3))
CHUNKS = C // P
PW, PH = W + 2, H + 2
TOTAL = IMAGES * UNITS

Q_LOW_AT = (2, 3)
BIAS_AT = 1
LAG_DW0, LAG_MID, LAG_DW1, LAG_OUT = 1, 2, 4, 6
BIASED_A, BIASED_V = 2, 1
BIASED = BIASED_A + BIASED_V
PEELED = -(-LAG_OUT // UNITS)

HALVES = 2
HROWS = HID // HALVES
HALF_C = C // HALVES
LOW_ROW = 32
BN = 3 + CHUNKS + 2
NBN = LAYERS * BN
TAPS = 9
COLS = 5 * NBN + LAYERS * TAPS
LATER_TAPS = TAPS - 1


def conv_stack_kernel(nc, x, cols, w1, w2, masks, ident, out):
    x_v = x.rearrange("n (u t r) w c -> (n u) (r w) t c", u=UNITS, t=TILES)
    out_v = out.rearrange("n (u t r) w c -> (n u) (r w) t c", u=UNITS, t=TILES)

    with ExitStack() as ctx:
        def sb(name, shape, dt=F32):
            return ctx.enter_context(nc.sbuf_tensor(name, shape, dt))

        def sem(name):
            return ctx.enter_context(nc.semaphore(name))

        x_sb = sb("x_sb", [TILE, UNITS, TILES, C])
        xt_sb = sb("xt_sb", [P, CHUNKS, UPIX])
        h_sb = [sb(f"h{n}_sb", [P, PH, PW]) for n in range(LAYERS)]
        acc_sb = [sb(f"acc{n}_sb", [P, 2, ROWS, W]) for n in range(LAYERS)]
        q_hi = [sb(f"q{n}_hi", [P, UPIX], F32R) for n in range(LAYERS)]
        stack = [sb(f"stack{n}", [P, n + 1, HALVES, UPIX], F32R) for n in range(LAYERS)]
        mid_sb = sb("mid_sb", [P, UNITS, CHUNKS, UPIX])
        out_sb = sb("out_sb", [P, 2, TILES, C])
        ident_sb = sb("ident_sb", [P, P])
        cols_sb = sb("cols_sb", [P, COLS])
        w1_sb = sb("w1_sb", [P, LAYERS, CHUNKS, HID // CHUNKS])
        w2_hi = sb("w2_hi", [P, LAYERS, C], F32R)
        w2_lo = sb("w2_lo", [P, LAYERS, C], F32R)
        scale_c = sb("scale_c", [P, NBN])
        shift_c = sb("shift_c", [P, NBN])
        tmp_c = sb("tmp_c", [P, NBN])
        taps_sb = sb("taps_sb", [P, LAYERS, TAPS])
        beta_sb = sb("beta_sb", [P, LAYERS])
        bias4_sb = sb("bias4_sb", [P, LAYERS, CHUNKS])
        bias_rows = sb("bias_rows", [P, C - P * BIASED], F32R)
        ones_rows = sb("ones_rows", [P, TILE], F32R)
        scratch = out_sb[:, :, :, :].rearrange("p s t c -> p (s t c)")
        place = [0]

        def carve(n):
            place[0] += n
            return scratch[:, place[0] - n:place[0]]

        var_c, inv_c, root_c = (carve(NBN) for _ in range(3))
        w2_in, masks_in = carve(LAYERS * HALVES * C // GROUPS), carve(GROUPS // HALVES + TILE)
        w2_f = carve(LAYERS * C)
        diag_sb = carve(LAYERS * C)
        ones_sb = carve(P)

        ps = ctx.enter_context(nc.psum_tensor("ps", [P, 8, 512], F32))

        x_loaded = [[sem(f"x_loaded_{u}_{part}") for part in range(2)] for u in range(UNITS)]
        params_loaded = sem("params_loaded")
        w1_loaded = sem("w1_loaded")
        w2_loaded = sem("w2_loaded")
        prep = sem("prep")
        roots = sem("roots")
        shifts_ready = sem("shifts_ready")
        diags_ready = sem("diags_ready")
        scales_spread = sem("scales_spread")
        w2_scaled = sem("w2_scaled")
        w2_split = sem("w2_split")
        bias_sums = sem("bias_sums")
        bias4_ready = sem("bias4_ready")
        bias_turned = sem("bias_turned")
        bias_split = sem("bias_split")
        weights_ready = sem("weights_ready")
        borders = sem("borders")
        blocks = sem("blocks")
        t0_filled = sem("t0_filled")
        xt_ready = sem("xt_ready")
        c1_filled = [sem(f"c1_{n}_filled") for n in range(LAYERS)]
        h_ready = [sem(f"h{n}_ready") for n in range(LAYERS)]
        tap0_done = [sem(f"tap0_{n}_done") for n in range(LAYERS)]
        taps_done = [sem(f"taps{n}_done") for n in range(LAYERS)]
        qh_ready = [sem(f"q{n}_hi_ready") for n in range(LAYERS)]
        ql_ready = [sem(f"q{n}_lo_ready") for n in range(LAYERS)]
        stacked = [[sem(f"stacked{n}_{k}") for k in range(n + 1)] for n in range(LAYERS)]
        mid_filled = sem("mid_filled")
        mid_ready = sem("mid_ready")
        mid_biased_a, mid_biased_v = sem("mid_biased_a"), sem("mid_biased_v")
        o_filled = sem("o_filled")
        o_ready = sem("o_ready")
        stored = [[sem(f"stored_{s}_{part}") for part in range(2)] for s in range(2)]

        STACKED = 16 * 2 * HALVES

        def stacked_wait(eng, n, v, u):
            if n == 0:
                eng.wait_ge(stacked[0][0], STACKED * (v + 1))
            else:
                eng.wait_ge(stacked[1][u % 2], STACKED * (v // 2 + 1))

        def span(part):
            first, n = PARTS[part]
            return first * TILE, (first + n) * TILE

        def active(s, lag):
            return not isinstance(s, int) or 0 <= s - lag < TOTAL

        def run_steps(eng, step, last, first=0):
            for s in range(first, PEELED * UNITS):
                step(s, s % UNITS, s // UNITS)
            with_tail = (last - TOTAL) // UNITS if last < TOTAL else 0
            end = IMAGES + with_tail
            with eng.Fori(PEELED, end) as i:
                for u in range(UNITS):
                    step(UNITS * i + u, u, i)
            for s in range(end * UNITS, TOTAL + LAG_OUT):
                step(s, s % UNITS, s // UNITS)

        block = ctx.enter_context(nc.Block())

        @block.sync
        def _(sp):
            def load(v, u):
                for part, (t, n) in enumerate(PARTS):
                    sp.dma_start(x_sb[:, u, t:t + n, :], x_v[v][:, t:t + n, :]).then_inc(x_loaded[u][part], 16)

            sp.dma_start(cols_sb[:, :], cols).then_inc(params_loaded, 16)
            sp.dma_start(ident_sb[:, :], ident).then_inc(params_loaded, 16)
            load(0, 0)
            sp.wait_ge(blocks, 2)
            half = P // 2
            for l in range(LAYERS):
                for t in range(2):
                    src = w1[l].rearrange("(c t) k d -> t k c d", t=2)[t]
                    sp.dma_start(w1_sb[half * t:half * (t + 1), l, :, 16 * t:16 * (t + 1)], src)\
                      .then_inc(w1_loaded, 16)
            sp.dma_start(w2_in, w2).then_inc(w2_loaded, 16)
            sp.dma_start(masks_in, masks).then_inc(w2_loaded, 16)
            load(1, 1)

            def store(z, s, u, part):
                sp.wait_ge(o_ready, TILES * z + PARTS[part][0] + PARTS[part][1])
                t, n = PARTS[part]
                sp.dma_start(out_v[z][:, t:t + n, :], out_sb[0:TILE, s, t:t + n, :]).then_inc(stored[s][part], 16)

            def stack_halves(n, y, uy):
                slot = uy % (n + 1)
                low = acc_sb[n][:, uy % 2, :, :].rearrange("p r w -> p (r w)")
                for k, (ready, src) in enumerate(((qh_ready[n], q_hi[n][:, :].bitcast(F32)), (ql_ready[n], low))):
                    sp.wait_ge(ready, y + 1)
                    for h in range(HALVES):
                        sp.dma_start(stack[n][HROWS * k:HROWS * (k + 1), slot, h, :].bitcast(F32), src[h::HALVES, :])\
                          .then_inc(stacked[n][slot], 16)

            def step(s, u, i):
                if active(s, LAG_OUT):
                    store(s - LAG_OUT, u % 2, u, 0)
                    store(s - LAG_OUT, u % 2, u, 1)
                if active(s, LAG_DW0):
                    stack_halves(0, s - LAG_DW0, (u - LAG_DW0) % UNITS)
                if active(s, LAG_DW1):
                    stack_halves(1, s - LAG_DW1, (u - LAG_DW1) % UNITS)
                if active(s, -2):
                    if active(s, LAG_MID):
                        sp.wait_ge(mid_filled, 8 * (s - LAG_MID + 1))
                    load(s + 2, (u + 2) % UNITS)

            run_steps(sp, step, TOTAL - UNITS)
            for s in range(2):
                for part in range(2):
                    sp.wait_ge(stored[s][part], 16 * (TOTAL // 2))

        @block.gpsimd
        def _(pool):
            nc.gpsimd.memset(w1_sb[:, :, :, :], 0.0).then_inc(blocks, 1)
            nc.gpsimd.memset(ones_sb, 1.0).then_inc(blocks, 1)
            for n in range(LAYERS):
                nc.gpsimd.memset(h_sb[n][:, :, :], 0.0).then_inc(borders, 1)

        @block.tensor
        def _(pe):
            def prepare():
                for l in range(LAYERS):
                    pe.wait_ge(diags_ready, l + 1)
                    pe.matmul(ps[:, 4 + l, :], ones_sb, diag_sb[:, C * l:C * (l + 1)], start=True, stop=True)\
                      .then_inc(scales_spread, 1)
                pe.wait_ge(w2_scaled, LAYERS)
                for l in range(LAYERS):
                    for c in range(CHUNKS):
                        h = P * c // HALF_C
                        rows = slice(HROWS * h, HROWS * (h + 1))
                        mm = pe.matmul(ps[:, 4 + h, CHUNKS * l + c:CHUNKS * l + c + 1],
                                       w2_f[rows, C * l + P * c:C * l + P * (c + 1)], beta_sb[rows, l:l + 1],
                                       start=True, stop=True, skip_group_check=True)
                mm.then_inc(bias_sums, 1)
                pe.wait_ge(bias4_ready, 1)
                for c in range(BIASED, CHUNKS):
                    tr = pe.transpose(ps[0:1, 4, P * (c - BIASED):P * (c - BIASED + 1)], bias4_sb[:, 1, c:c + 1],
                                      ident_sb[:, :])
                tr.then_inc(bias_turned, 1)

            def transpose_item(s, u, i, j):
                part, cp = divmod(j, 2)
                if cp == 0:
                    pe.wait_ge(x_loaded[u][part], 16 * (i + 1))
                if j >= 2:
                    pe.wait_ge(xt_ready, 4 * s + j - 1)
                elif active(s, LAG_MID + 1):
                    pe.wait_ge(mid_ready, 8 * (s - LAG_MID - 1) + 2 * (j + 3))
                elif active(s, 1):
                    pe.wait_ge(xt_ready, 4 * (s - 1) + j + 3)
                first, n = PARTS[part]
                for k in range(2):
                    c = 2 * cp + k
                    for t in range(n):
                        tr = pe.transpose(ps[:, 2 * (j % 2) + k, TILE * t:TILE * (t + 1)],
                                          x_sb[:, u, first + t, P * c:P * (c + 1)], ident_sb[0:TILE, 0:TILE])
                tr.then_inc(t0_filled, 1)

            def conv1(n, v, part, src, ready, per_part, bank_free):
                pe.wait_ge(ready, 2 * per_part * v + per_part * (part + 1))
                if bank_free is not None:
                    pe.wait_ge(bank_free[0], bank_free[1] + part + 1)
                a, b = span(part)
                for c in range(CHUNKS):
                    mm = pe.matmul(ps[32 * c:32 * (c + 1), 6 + part, 0:b - a], w1_sb[:, n, c, :],
                                   src[:, c, a:b], start=True, stop=True)
                mm.then_inc(c1_filled[n], 1)

            def conv1_mid(s, u, part, lag):
                w = s - lag
                if active(s, lag - LAG_MID):
                    free = (h_ready[0], 2 * (s - lag + LAG_MID))
                else:
                    free = (h_ready[1], 2 * (w - 1))
                conv1(1, w, part, mid_sb[:, (u - lag) % UNITS, :, :], mid_ready, 4, free)

            def mid_item(s, u, j):
                w = s - LAG_MID
                uw = (u - LAG_MID) % UNITS
                part, cp = divmod(j, 2)
                if j == 0:
                    stacked_wait(pe, 0, w, uw)
                if j >= 2:
                    pe.wait_ge(mid_ready, 8 * w + 2 * (j - 1))
                elif active(s, 0):
                    pe.wait_ge(xt_ready, 4 * s + j + 3)
                else:
                    pe.wait_ge(mid_ready, 8 * (w - 1) + 2 * (j + 3))
                a, b = span(part)
                first, n = PARTS[part]
                for k in range(2):
                    c = 2 * cp + k
                    bank = 2 * (j % 2) + k
                    for wt in (w2_hi, w2_lo):
                        pe.matmul(ps[:, bank, 0:b - a], wt[:, 0, P * c:P * (c + 1)],
                                  stack[0][:, 0, P * c // HALF_C, a:b], start=(wt is w2_hi), stop=(wt is w2_lo))
                    for t in range(n):
                        tr = pe.matmul(ps[:, bank, TILE * t:TILE * (t + 1)],
                                       x_sb[:, uw, first + t, P * c:P * (c + 1)], ident_sb[0:TILE, 0:TILE],
                                       start=False, stop=True, is_transpose=True, skip_group_check=True)
                    tr.then_inc(mid_filled, 1)

            def out_tile(s, u, t):
                z = s - LAG_OUT
                uz = (u - LAG_OUT) % UNITS
                bank = 4 + (u + t) % 2
                if t == 0:
                    stacked_wait(pe, 1, z, uz)
                    pe.wait_ge(mid_biased_a, BIASED_A * (z + 1))
                    pe.wait_ge(mid_biased_v, BIASED_V * (z + 1))
                if not isinstance(z, int) or z > 0 or t >= 2:
                    pe.wait_ge(o_ready, TILES * z + t - 1)
                cut = slice(TILE * t, TILE * (t + 1))
                for h in range(HALVES):
                    cols_h = slice(HALF_C * h, HALF_C * (h + 1))
                    for wt in (w2_hi, w2_lo):
                        pe.matmul(ps[0:TILE, bank, cols_h], stack[1][:, uz % 2, h, cut], wt[:, 1, cols_h],
                                  start=(h == 0 and wt is w2_hi), stop=(wt is w2_lo), skip_group_check=True)
                pe.matmul(ps[0:TILE, bank, P * BIASED:], ones_rows[:, :], bias_rows[:, :],
                          start=False, stop=True, skip_group_check=True)
                for c in range(CHUNKS):
                    tr = pe.matmul(ps[0:TILE, bank, P * c:P * (c + 1)], mid_sb[:, uz, c, cut], ident_sb[:, :],
                                   start=False, stop=True, is_transpose=True, skip_group_check=True)
                tr.then_inc(o_filled, 1)

            def step(s, u, i):
                here, mid, late = active(s, 0), active(s, LAG_MID), active(s, LAG_OUT)
                behind_mid = active(s, LAG_MID + 1)
                if behind_mid:
                    free = (h_ready[1], 2 * (s - LAG_MID - 1))
                else:
                    free = (h_ready[0], 2 * (s - 1)) if active(s, 1) else None
                if behind_mid:
                    conv1_mid(s, u, 1, LAG_MID + 1)
                if here:
                    transpose_item(s, u, i, 0)
                if late:
                    out_tile(s, u, 0)
                if here:
                    transpose_item(s, u, i, 1)
                if late:
                    out_tile(s, u, 1)
                    out_tile(s, u, 2)
                if here:
                    transpose_item(s, u, i, 2)
                    transpose_item(s, u, i, 3)
                if late:
                    out_tile(s, u, 3)
                    out_tile(s, u, 4)
                if here:
                    conv1(0, s, 0, xt_sb, xt_ready, 2, free)
                    conv1(0, s, 1, xt_sb, xt_ready, 2, free)
                if late:
                    out_tile(s, u, 5)
                if mid:
                    mid_item(s, u, 0)
                    mid_item(s, u, 1)
                if late:
                    out_tile(s, u, 6)
                if mid:
                    mid_item(s, u, 2)
                    mid_item(s, u, 3)
                    conv1_mid(s, u, 0, LAG_MID)

            pe.wait_ge(params_loaded, 16 * 2)
            pe.wait_ge(w1_loaded, 16 * 2 * LAYERS)
            step(0, 0, 0)
            prepare()
            pe.wait_ge(weights_ready, 1)
            run_steps(pe, step, TOTAL, 1)

        @block.scalar
        def _(act):
            act.wait_ge(prep, 2)
            nc.scalar.activation(root_c, inv_c, ACT.Sqrt).then_inc(roots, 1)

            def x_item(s, j):
                part, cp = divmod(j, 2)
                act.wait_ge(t0_filled, 4 * s + j + 1)
                if cp == 0 and active(s, 1):
                    act.wait_ge(c1_filled[0], 2 * (s - 1) + part + 1)
                a, b = span(part)
                pair = 2 * (j % 2)
                nc.scalar.copy(xt_sb[:, 2 * cp:2 * cp + 2, a:b], ps[:, pair:pair + 2, 0:b - a]).then_inc(xt_ready, 1)

            def h_part(n, v, uv, part, old):
                act.wait_ge(c1_filled[n], 2 * v + part + 1)
                if old:
                    act.wait_ge(taps_done[n], LATER_TAPS * (v - 2))
                a, b = span(part)
                r0 = 1 + ROWS * uv + a // W
                nc.scalar.activation(
                    h_sb[n][:, r0:r0 + (b - a) // W, 1:1 + W],
                    ps[:, 6 + part, 0:b - a].rearrange("p (r w) -> p r w", w=W),
                    ACT.Relu, scale=scale_c[:, BN * n:BN * n + 1],
                    bias=shift_c[:, BN * n:BN * n + 1]).then_inc(h_ready[n], 1)

            def h1_part(s, u, part, lag):
                h_part(1, s - lag, (u - lag) % UNITS, part, active(s, lag + 3))

            def mid_item(s, u, j):
                w = s - LAG_MID
                uw = (u - LAG_MID) % UNITS
                part, cp = divmod(j, 2)
                if cp == 0 and active(s, LAG_OUT):
                    act.wait_ge(o_filled, TILES * (w - 4) + PARTS[part][0] + PARTS[part][1])
                a, b = span(part)
                for k in range(2):
                    c = 2 * cp + k
                    act.wait_ge(mid_filled, 8 * w + 2 * j + k + 1)
                    nc.scalar.activation(mid_sb[:, uw, c, a:b], ps[:, 2 * (j % 2) + k, 0:b - a], ACT.Relu,
                                         bias=bias4_sb[:, 0, c:c + 1]).then_inc(mid_ready, 1)

            def add_bias(s, u, c):
                w = s - LAG_MID - 1
                uw = (u - LAG_MID - 1) % UNITS
                act.wait_ge(c1_filled[1], 2 * w + 2)
                act.wait_ge(mid_ready, 8 * w + 8)
                nc.scalar.activation(mid_sb[:, uw, c, :], mid_sb[:, uw, c, :], ACT.Identity,
                                     bias=bias4_sb[:, 1, c:c + 1]).then_inc(mid_biased_a, 1)

            def q_high(n, y, uy, units_before):
                act.wait_ge(taps_done[n], LATER_TAPS * (y + 1))
                if n == 0 and units_before >= 1:
                    act.wait_ge(mid_filled, 8 * y)
                if n == 1 and units_before >= 1:
                    stacked_wait(act, 1, y - 1, uy - 1)
                if n == 1 and units_before >= 2:
                    act.wait_ge(o_filled, TILES * (y - 1))
                nc.scalar.copy(q_hi[n][:, :], acc_sb[n][:, uy % 2, :, :].rearrange("p r w -> p (r w)"))\
                  .then_inc(qh_ready[n], 1)

            def tap0(n, y, uy, old):
                act.wait_ge(h_ready[n], 2 * (y + 1))
                if old:
                    stacked_wait(act, n, y - 2, uy)
                nc.scalar.activation(acc_sb[n][:, uy % 2, :, :], h_sb[n][:, ROWS * uy:ROWS * (uy + 1), 0:W], ACT.Copy,
                                     scale=taps_sb[:, n, 0:1]).then_inc(tap0_done[n], 1)

            def out_tile(s, u, t):
                z = s - LAG_OUT
                slot = u % 2
                act.wait_ge(o_filled, TILES * z + t + 1)
                for part in range(2):
                    if t == PARTS[part][0] and active(s, LAG_OUT + 2):
                        act.wait_ge(stored[slot][part], stores_before(s, u) * 16)
                nc.scalar.activation(out_sb[0:TILE, slot, t, :], ps[0:TILE, 4 + (u + t) % 2, :], ACT.Relu)\
                  .then_inc(o_ready, 1)

            def stores_before(s, u):
                if isinstance(s, int):
                    return (s - LAG_OUT) // 2
                return image[0] * (UNITS // 2) + (u - LAG_OUT) // 2

            image = [None]

            def step(s, u, i):
                image[0] = i
                here, mid, late = active(s, 0), active(s, LAG_MID), active(s, LAG_OUT)
                behind_mid = active(s, LAG_MID + 1)
                if behind_mid:
                    h1_part(s, u, 1, LAG_MID + 1)
                if active(s, 1 + LAG_DW0):
                    y = s - 1 - LAG_DW0
                    q_high(0, y, (u - 1 - LAG_DW0) % UNITS, 2 if active(s, 3 + LAG_DW0) else y)
                if here:
                    x_item(s, 0)
                if late:
                    out_tile(s, u, 0)
                if active(s, 1 + LAG_DW1):
                    y = s - 1 - LAG_DW1
                    q_high(1, y, (u - 1 - LAG_DW1) % UNITS, 2 if active(s, 3 + LAG_DW1) else y)
                if here:
                    x_item(s, 1)
                if late:
                    out_tile(s, u, 1)
                    out_tile(s, u, 2)
                if here:
                    x_item(s, 2)
                    x_item(s, 3)
                if late:
                    out_tile(s, u, 3)
                    out_tile(s, u, 4)
                if behind_mid:
                    add_bias(s, u, 0)
                if here:
                    h_part(0, s, u, 0, active(s, 3))
                    h_part(0, s, u, 1, active(s, 3))
                    tap0(0, s, u, active(s, 2))
                if late:
                    out_tile(s, u, 5)
                if mid:
                    mid_item(s, u, 0)
                    mid_item(s, u, 1)
                if behind_mid:
                    tap0(1, s - LAG_MID - 1, (u - LAG_MID - 1) % UNITS, active(s, LAG_MID + 3))
                if late:
                    out_tile(s, u, 6)
                if mid:
                    mid_item(s, u, 2)
                    mid_item(s, u, 3)
                if behind_mid:
                    add_bias(s, u, 1)
                if mid:
                    h1_part(s, u, 0, LAG_MID)

            act.wait_ge(shifts_ready, 1)
            act.wait_ge(borders, LAYERS)
            for s in range(2):
                step(s, s, 0)
            act.wait_ge(weights_ready, 1)
            run_steps(act, step, TOTAL, 2)

        @block.vector
        def _(dve):
            done = [0]

            def then(ins):
                done[0] += 1
                ins.then_inc(prep, 1)
                dve.wait_ge(prep, done[0])

            dve.wait_ge(params_loaded, 16 * 2)
            var, gamma, mean, beta, conv_bias = (cols_sb[:, NBN * k:NBN * (k + 1)] for k in range(5))
            then(nc.vector.tensor_scalar(var_c, var, EPS, None, ALU.add))
            then(nc.vector.reciprocal(inv_c, var_c))
            dve.wait_ge(roots, 1)
            then(nc.vector.reciprocal(var_c, root_c))
            then(nc.vector.tensor_tensor(var_c, var_c, inv_c, ALU.mult))
            then(nc.vector.tensor_tensor(root_c, root_c, var_c, ALU.add))
            then(nc.vector.scalar_tensor_tensor(out=scale_c[:, :], in0=root_c, scalar=0.5, in1=gamma,
                                                op0=ALU.mult, op1=ALU.mult))
            then(nc.vector.tensor_tensor(tmp_c[:, :], conv_bias, mean, ALU.subtract))
            then(nc.vector.tensor_tensor(tmp_c[:, :], tmp_c[:, :], scale_c[:, :], ALU.mult))
            then(nc.vector.tensor_tensor(shift_c[:, :], tmp_c[:, :], beta, ALU.add))
            for l in range(LAYERS):
                b2, b3 = BN * l + 1, BN * l + 2
                s2, s3 = BN * l + BN - 2, BN * l + BN - 1
                raw = cols_sb[:, 5 * NBN + TAPS * l:5 * NBN + TAPS * (l + 1)]
                nc.vector.tensor_scalar(taps_sb[:, l, :], raw, scale_c[:, b2:b2 + 1], scale_c[:, b3:b3 + 1],
                                        ALU.mult, ALU.mult)
                last = nc.vector.tensor_scalar(beta_sb[:, l:l + 1], shift_c[:, s2:s2 + 1], scale_c[:, s3:s3 + 1],
                                               shift_c[:, s3:s3 + 1], ALU.mult, ALU.add)
            last.then_inc(shifts_ready, 1)
            dve.wait_ge(blocks, 2)
            for l in range(LAYERS):
                for c in range(CHUNKS):
                    scale = scale_c[:, BN * l + 3 + c:BN * l + 4 + c]
                    last = nc.vector.tensor_scalar(diag_sb[:, C * l + P * c:C * l + P * (c + 1)], ident_sb[:, :],
                                                   scale, None, ALU.mult)
                last.then_inc(diags_ready, 1)
            dve.wait_ge(w2_loaded, 16 * 2)
            per = C // GROUPS
            for l in range(LAYERS):
                for g in range(GROUPS):
                    h, k = divmod(g, GROUPS // HALVES)
                    src = w2_in[:, per * (HALVES * l + h):per * (HALVES * l + h + 1)]
                    last = nc.vector.tensor_scalar(w2_f[:, C * l + per * g:C * l + per * (g + 1)], src,
                                                   masks_in[:, k:k + 1], None, ALU.mult)
            then(last)
            for l in range(LAYERS):
                dve.wait_ge(scales_spread, l + 1)
                nc.vector.tensor_tensor(w2_f[:, C * l:C * (l + 1)], w2_f[:, C * l:C * (l + 1)], ps[:, 4 + l, :],
                                        ALU.mult).then_inc(w2_scaled, 1)
            dve.wait_ge(w2_scaled, LAYERS)
            high, low = (w[:, :, :].rearrange("p l c -> p (l c)") for w in (w2_hi, w2_lo))
            nc.vector.tensor_copy(high, w2_f).then_inc(w2_split, 1)
            dve.wait_ge(bias_sums, 1)
            for l in range(LAYERS):
                for h in range(HALVES):
                    c0, c1 = CHUNKS // HALVES * h, CHUNKS // HALVES * (h + 1)
                    last = nc.vector.tensor_tensor(
                        bias4_sb[:, l, c0:c1], ps[:, 4 + h, CHUNKS * l + c0:CHUNKS * l + c1],
                        shift_c[:, BN * l + 3 + c0:BN * l + 3 + c1], ALU.add)
            last.then_inc(bias4_ready, 1)
            dve.wait_ge(w2_split, 1)
            nc.vector.tensor_tensor(low, w2_f, high.bitcast(F32), ALU.subtract)
            then(nc.vector.memset(bias_rows[:, :].bitcast(F32), 0.0))
            nc.vector.tensor_copy(ones_rows[:, :], masks_in[:, GROUPS // HALVES:])
            dve.wait_ge(bias_turned, 1)
            turned = ps[0:1, 4, 0:C - P * BIASED]
            nc.vector.tensor_copy(bias_rows[0:1, :], turned).then_inc(bias_split, 1)
            dve.wait_ge(bias_split, 1)
            nc.vector.tensor_tensor(bias_rows[LOW_ROW:LOW_ROW + 1, :], turned, bias_rows[0:1, :].bitcast(F32),
                                    ALU.subtract).then_inc(weights_ready, 1)

            def tap(n, y, uy, k):
                dy, dx = divmod(k, 3)
                window = h_sb[n][:, ROWS * uy + dy:ROWS * uy + dy + ROWS, dx:dx + W]
                total = acc_sb[n][:, uy % 2, :, :]
                if k == 1:
                    dve.wait_ge(tap0_done[n], y + 1)
                else:
                    dve.wait_ge(taps_done[n], LATER_TAPS * y + k - 1)
                nc.vector.scalar_tensor_tensor(out=total, in0=window, scalar=taps_sb[:, n, k:k + 1], in1=total,
                                               op0=ALU.mult, op1=ALU.add).then_inc(taps_done[n], 1)

            def add_bias(uy, c):
                chunk = mid_sb[:, uy, c, :]
                nc.vector.tensor_scalar(chunk, chunk, bias4_sb[:, 1, c:c + 1], None, ALU.add).then_inc(mid_biased_v, 1)

            def q_low(n, y, uy):
                dve.wait_ge(qh_ready[n], y + 1)
                total = acc_sb[n][:, uy % 2, :, :].rearrange("p r w -> p (r w)")
                nc.vector.tensor_tensor(total.bitcast(F32R), total, q_hi[n][:, :].bitcast(F32), ALU.subtract)\
                  .then_inc(ql_ready[n], 1)

            def step(s, u, i):
                on = [active(s, LAG_DW0), active(s, LAG_DW1)]
                ys = [s - LAG_DW0, s - LAG_DW1]
                us = [(u - LAG_DW0) % UNITS, (u - LAG_DW1) % UNITS]
                below = [1 if v < UNITS - 1 else 0 for v in us]
                for k in range(1, TAPS):
                    for n in range(LAYERS):
                        if on[n]:
                            if k == TAPS - 3:
                                dve.wait_ge(h_ready[n], 2 * (ys[n] + 1) + below[n])
                            tap(n, ys[n], us[n], k)
                        if n == 1 and on[n] and k == BIAS_AT:
                            for c in range(BIASED_A, BIASED):
                                add_bias(us[n], c)
                        if k == Q_LOW_AT[n] and active(s, (LAG_DW0, LAG_DW1)[n] + 1):
                            q_low(n, ys[n] - 1, (us[n] - 1) % UNITS)

            run_steps(dve, step, TOTAL)


_BNS = [(1, "b1"), (2, "dw_b"), (3, None), (4, "b2")]


PER_GROUP = HID // GROUPS


def _halves(v):
    return v.reshape(GROUPS, HALVES, PER_GROUP // HALVES, *v.shape[1:]).swapaxes(1, 2).reshape(v.shape)


def _hidden(v):
    return v.reshape(HALVES, PER_GROUP // HALVES, GROUPS, *v.shape[1:]).swapaxes(0, 2).reshape(v.shape)


def _stacked(v):
    return v.reshape(HALVES, PER_GROUP // HALVES, GROUPS, *v.shape[1:]).swapaxes(1, 2).reshape(v.shape)


def _columns(inputs, what):
    cols = []
    for l in range(LAYERS):
        v = {}
        for n, conv_bias in _BNS:
            name = f"bn{n}_{what}" if what else conv_bias
            v[n] = np.asarray(inputs[f"L{l}_conv_{name}"]) if name else np.zeros(HID, np.float32)
        cols += [_halves(v[1]), _hidden(v[2]), _hidden(v[3]), *v[4].reshape(-1, P), _stacked(v[2]), _stacked(v[3])]
    return cols


def kernel(**inputs):
    import concourse.bacc as bacc
    from concourse.bass_utils import run_bass_kernel_spmd

    cols = [c for what in ("v", "g", "m", "b", None) for c in _columns(inputs, what)]
    for l in range(LAYERS):
        cols += list(_hidden(np.asarray(inputs[f"L{l}_conv_dw_w"]).reshape(TAPS, HID).T).T)
    w1 = np.stack([np.asarray(inputs[f"L{l}_conv_w1"]) for l in range(LAYERS)])
    w1 = w1.reshape(LAYERS, GROUPS, C // GROUPS, HALVES, -1).swapaxes(3, 4).reshape(w1.shape)
    w2 = [_stacked(np.asarray(inputs[f"L{l}_conv_w2"]).reshape(HID, C // GROUPS))[HROWS * h:HROWS * (h + 1)]
          for l in range(LAYERS) for h in range(HALVES)]
    w2 = np.tile(np.concatenate(w2, axis=1), (2, 1))
    group = _stacked(np.arange(HID) // PER_GROUP) % (GROUPS // HALVES)
    ones = np.zeros((P, TILE), np.float32)
    ones[[0, LOW_ROW]] = 1
    arrays = {
        "x": np.ascontiguousarray(inputs["x"]),
        "cols": np.ascontiguousarray(np.stack(cols, axis=1)),
        "w1": np.ascontiguousarray(w1),
        "w2": np.ascontiguousarray(w2),
        "masks": np.concatenate([group[:, None] == np.arange(GROUPS // HALVES), ones], axis=1).astype(np.float32),
        "ident": np.eye(P, dtype=np.float32),
    }
    nc = bacc.Bacc("TRN2", target_bir_lowering=False, num_devices=1, dynamic_dma_scratch_size=1024)
    aps = [nc.dram_tensor(n, a.shape, mybir.dt.from_np(a.dtype), kind="ExternalInput").ap() for n, a in arrays.items()]
    out = nc.dram_tensor("out", (IMAGES, H, W, C), F32, kind="ExternalOutput").ap()
    conv_stack_kernel(nc, *aps, out)
    r = run_bass_kernel_spmd(nc, [arrays], core_ids=[0])
    return r.results[0]["out"]
```
